# Optimizing a Trainium2 kernel written in Bass

```python
import numpy as np
import jax
import jax.numpy as jnp

def _softmax(x, axis=-1):
    return jax.nn.softmax(x, axis=axis)

def _gelu(x):
    return jax.nn.gelu(x, approximate=True)

def _silu(x):
    return jax.nn.silu(x)

def _sigmoid(x):
    return jax.nn.sigmoid(x)

def _layernorm(x, axis=-1, eps=1e-05):
    m = jnp.mean(x, axis=axis, keepdims=True)
    v = jnp.var(x, axis=axis, keepdims=True)
    return (x - m) / jnp.sqrt(v + eps)

def _scatter_add(tgt, idx, src, axis=0):
    return tgt.at[idx].add(src)

def _segment_sum(src, seg, n):
    return jax.ops.segment_sum(src, seg, n)
kernel_name = 'mk_cond_resid_d2_seqx_r8_b25720'

def setup_inputs(seed: int=0):
    np.random.seed(seed)
    _w = jnp.asarray

    def _rec_inputs():
        import jax
        import jax.numpy as jnp
        _rk = jax.random.key(seed)
        x = -0.000125 + 0.9999 * jax.random.normal(jax.random.fold_in(_rk, 1), (32, 32, 512), jnp.float32)
        _lenS = 32 - jax.random.randint(jax.random.fold_in(_rk, 7), (32,), 0, max(1, 32 // 4) + 1, jnp.int32)
        _lenS2 = 32 - jax.random.randint(jax.random.fold_in(_rk, 8), (32,), 0, max(1, 32 // 4) + 1, jnp.int32)
        itok_B_0_7 = jax.random.randint(jax.random.fold_in(_rk, 11), (32,), 0, 8, jnp.int32)
        itok_B_2_6 = jax.random.randint(jax.random.fold_in(_rk, 12), (32,), 2, 7, jnp.int32)
        return (x, itok_B_0_7, itok_B_2_6)
    x, itok_B_0_7, itok_B_2_6 = _rec_inputs()

    def _L0_cond_setup():
        import jax, jax.numpy as jnp
        import numpy as np
        TOP_K = 2
        LANG_BIAS = 5.0
        SCALING = 32.0 / 16.0
        LANGUAGE_PAD_ID = -1
        key = jax.random.key(seed)
        ks = jax.random.split(key, 6)
        B, T, D, O, E, R = (4, 256, 512, 512, 8, 16)
        x = jax.random.normal(ks[0], (B, T, D), dtype=jnp.float32)
        language_ids = jax.random.randint(ks[1], (B,), 0, E).astype(jnp.int64)
        W = jax.random.normal(ks[2], (O, D), dtype=jnp.float32) * (1.0 / np.sqrt(D))
        Wr = jax.random.normal(ks[3], (E, D), dtype=jnp.float32) * (1.0 / np.sqrt(D))
        A = jax.random.normal(ks[4], (E, R, D), dtype=jnp.float32) * (1.0 / np.sqrt(D))
        Bm = jax.random.normal(ks[5], (O, R), dtype=jnp.float32) * 0.0
        Bm = jnp.broadcast_to(Bm, (E, O, R)) + jax.random.normal(ks[5], (E, O, R), dtype=jnp.float32) * 0.02
        return {'x': x, 'language_ids': language_ids, 'W': W, 'Wr': Wr, 'A': A, 'B': Bm}
    _L0_cond_all = _L0_cond_setup()
    _L0_cond_in = {k: v for k, v in _L0_cond_all.items() if k in ('W', 'Wr', 'A', 'B')}
    del _L0_cond_all

    def _L1_cond_setup():
        import jax, jax.numpy as jnp
        import numpy as np
        B, N, H, F = (4, 64, 512, 1376)
        L, R, RANK = (1, 16, 16)
        SCALE = 0.5
        key = jax.random.key(seed)
        ks = jax.random.split(key, 12)
        nrm = lambda k, shape, fan: jax.random.normal(k, shape, jnp.float32) * fan ** (-0.5)
        inp = {'x': jax.random.normal(ks[0], (B, N, H), jnp.float32), 'W_gate': nrm(ks[1], (F, H), H), 'W_up': nrm(ks[2], (F, H), H), 'W_down': nrm(ks[3], (H, F), F), 'A_gate': nrm(ks[4], (L, R, RANK, H), H), 'B_gate': nrm(ks[5], (L, R, F, RANK), RANK), 'A_up': nrm(ks[6], (L, R, RANK, H), H), 'B_up': nrm(ks[7], (L, R, F, RANK), RANK), 'A_down': nrm(ks[8], (L, R, RANK, F), F), 'B_down': nrm(ks[9], (L, R, H, RANK), RANK), 'lora_indices': jax.random.randint(ks[10], (B,), 0, R), 'layer_idx': 0}
        return inp
    _L1_cond_all = _L1_cond_setup()
    _L1_cond_in = {k: v for k, v in _L1_cond_all.items() if k in ('W_gate', 'W_up', 'W_down', 'A_gate', 'B_gate', 'A_up', 'B_up', 'A_down', 'B_down')}
    del _L1_cond_all
    return {'x': x, 'itok_B_0_7': itok_B_0_7, 'itok_B_2_6': itok_B_2_6, 'L0_cond_W': _L0_cond_in['W'], 'L0_cond_Wr': _L0_cond_in['Wr'], 'L0_cond_A': _L0_cond_in['A'], 'L0_cond_B': _L0_cond_in['B'], 'L1_cond_W_gate': _L1_cond_in['W_gate'], 'L1_cond_W_up': _L1_cond_in['W_up'], 'L1_cond_W_down': _L1_cond_in['W_down'], 'L1_cond_A_gate': _L1_cond_in['A_gate'], 'L1_cond_B_gate': _L1_cond_in['B_gate'], 'L1_cond_A_up': _L1_cond_in['A_up'], 'L1_cond_B_up': _L1_cond_in['B_up'], 'L1_cond_A_down': _L1_cond_in['A_down'], 'L1_cond_B_down': _L1_cond_in['B_down']}

def reference(x, itok_B_0_7, itok_B_2_6, L0_cond_W, L0_cond_Wr, L0_cond_A, L0_cond_B, L1_cond_W_gate, L1_cond_W_up, L1_cond_W_down, L1_cond_A_gate, L1_cond_B_gate, L1_cond_A_up, L1_cond_B_up, L1_cond_A_down, L1_cond_B_down):
    import jax
    import jax.numpy as jnp

    def _L0_cond_ref(x, language_ids, W, Wr, A, B):
        import jax, jax.numpy as jnp
        import numpy as np
        TOP_K = 2
        LANG_BIAS = 5.0
        SCALING = 32.0 / 16.0
        LANGUAGE_PAD_ID = -1
        base = jnp.einsum('btd,od->bto', x, W)
        E = Wr.shape[0]
        logits = jnp.einsum('btd,ed->bte', x.astype(jnp.float32), Wr.astype(jnp.float32))
        expert_targets = language_ids
        valid = expert_targets >= 0
        tgt = jnp.where(valid, expert_targets, 0)
        bias = jax.nn.one_hot(tgt, E, dtype=logits.dtype) * LANG_BIAS
        bias = jnp.where(valid[:, None], bias, 0.0)
        logits = logits + bias[:, None, :]
        topw, topi = jax.lax.top_k(logits, TOP_K)
        weights = jax.nn.softmax(topw, axis=-1)
        gates = jnp.sum(jax.nn.one_hot(topi, E, dtype=weights.dtype) * weights[..., None], axis=-2)
        gates = gates.astype(x.dtype)
        h = jnp.einsum('btd,erd->bter', x, A)
        lora_out = jnp.einsum('bter,bte,eor->bto', h, gates, B)
        return base + SCALING * lora_out

    def _L1_cond_ref(x, W_gate, W_up, W_down, A_gate, B_gate, A_up, B_up, A_down, B_down, lora_indices, layer_idx):
        import jax, jax.numpy as jnp
        import numpy as np
        B, N, H, F = (4, 64, 512, 1376)
        L, R, RANK = (1, 16, 16)
        SCALE = 0.5

        def lora_add(base, inp, A, B):
            Ab = A[layer_idx][lora_indices]
            Bb = B[layer_idx][lora_indices]
            t = jnp.einsum('bri,bni->bnr', Ab, inp)
            return base + jnp.einsum('bor,bnr->bno', Bb, t) * SCALE
        gate = lora_add(jnp.einsum('bnh,fh->bnf', x, W_gate), x, A_gate, B_gate)
        up = lora_add(jnp.einsum('bnh,fh->bnf', x, W_up), x, A_up, B_up)
        act = jax.nn.silu(gate) * up
        down = lora_add(jnp.einsum('bnf,hf->bnh', act, W_down), act, A_down, B_down)
        return down
    x = x + _L0_cond_ref(x, itok_B_0_7, L0_cond_W, L0_cond_Wr, L0_cond_A, L0_cond_B)
    x = x + _L1_cond_ref(x, L1_cond_W_gate, L1_cond_W_up, L1_cond_W_down, L1_cond_A_gate, L1_cond_B_gate, L1_cond_A_up, L1_cond_B_up, L1_cond_A_down, L1_cond_B_down, itok_B_2_6, 0)
    return x

_drawn_inputs = setup_inputs


def setup_inputs(seed=0):
    import zlib

    import numpy as np

    out = dict(_drawn_inputs(seed))
    spreads = {}
    factors = {'L0_cond_Wr': 4.125}
    for name, (base, spread) in spreads.items():
        noise = np.random.default_rng([zlib.crc32(name.encode()), seed]).standard_normal(out[name].shape)
        drawn = base * np.exp(spread * noise) if base else spread * noise
        out[name] = jnp.asarray(drawn.astype(out[name].dtype))
    for name, factor in factors.items():
        out[name] = (out[name] * factor).astype(out[name].dtype)
    return out
```

```python
from contextlib import ExitStack

import concourse.bass as bass
from concourse import mybir

ALU = mybir.AluOpType
ACT = mybir.ActivationFunctionType
F32 = mybir.dt.float32
F32R = mybir.dt.float32r
I32 = mybir.dt.int32
U32 = mybir.dt.uint32

P = 128
TOKENS = 1024
HALF = 512
NH = TOKENS // HALF
D = 512
KT = D // P
E0, R0 = 8, 16
ER0 = E0 * R0
HC = ER0 + E0
LANG_BIAS = 5.0
SCALING = 2.0
TT = HALF // P
E1, R1 = 16, 16
F = 1376
FT = -(-F // P)
F_LAST = F - (FT - 1) * P
BATCH_TOKENS = 32
GB = P // R1
GT = GB * BATCH_TOKENS
NG = TOKENS // GT
GH = NG // NH
GW = 3 * P
HSTEPS = NH * FT

C_MASK, C_ID, C_IOTA, C_FTOFF, C_ROFF = 0, GT, GT + P, GT + P + E0, GT + P + E0 + FT * NG
C_END = C_ROFF + 1


def mlp_with_loras(nc, xT, w0T, ar0T, b0T, consts, ids, wgu, a_rows, ft_rows, wd, bd_rows, out):
    with ExitStack() as ctx:
        def sem(name):
            return ctx.enter_context(nc.semaphore(name))

        cursor = [-(-nc.sbuf_base // 32) * 32]

        def region(nbytes):
            at = cursor[0]
            cursor[0] += -(-nbytes // 32) * 32
            return at

        def place(name, shape, dt, at):
            return nc.alloc_sbuf_tensor_at(name, shape, dt, offset=at)

        KB = 1024
        r_act = region(FT * TOKENS * 8)
        r_x1 = region(KT * TOKENS * 8)
        r_wraw = region(8 * KB)
        r_graw = region(2 * NG * GW * 4)
        r_wsp = region(16 * KB)
        r_bsp1 = region(8 * KB)
        r_bsp0 = region(8 * KB)
        r_asp = region(8 * KB)
        r_t = region(16 * KB)
        r_misc = region(8 * KB)

        x_raw = [place(f"x_raw{h}", [P, KT, HALF], F32, r_act + h * 8 * KB) for h in range(NH)]
        x_hi = [place(f"x_hi{h}", [P, KT, HALF], F32R, r_act + (16 + 8 * h) * KB) for h in range(NH)]
        x_lo = [place(f"x_lo{h}", [P, KT, HALF], F32R, r_act + (32 + 8 * h) * KB) for h in range(NH)]
        w0_hi = place("w0_hi", [P, KT, D], F32R, r_act + 48 * KB)
        w0_lo = place("w0_lo", [P, KT, D], F32R, r_act + 56 * KB)
        w0_raw = place("w0_raw", [P, KT, D], F32, r_act + 64 * KB)
        ghT_hi = place("ghT_hi", [P, TOKENS], F32R, r_act + 72 * KB)
        ghT_lo = place("ghT_lo", [P, TOKENS], F32R, r_act + 76 * KB)
        AR = KT * HC * 4
        ar_raw = place("ar_raw", [P, KT, HC], F32, r_act + 80 * KB)
        ar_hi = place("ar_hi", [P, KT, HC], F32R, r_act + 80 * KB + AR)
        ar_lo = place("ar_lo", [P, KT, HC], F32R, r_act + 80 * KB + 2 * AR)
        at_shape = [P, GH, 2, KT * P]
        at_hi = [place("at_hi0", at_shape, F32R, r_act + 64 * KB), place("at_hi1", at_shape, F32R, r_act + 16 * KB)]
        at_lo = [place("at_lo0", at_shape, F32R, r_misc), place("at_lo1", at_shape, F32R, r_act + 32 * KB)]
        a_raw = place("a_raw", [P, NG, 2 * D], F32, r_t)
        b0_raw = place("b0_raw", [P, D], F32, r_bsp1)
        b0_hi = place("b0_hi", [P, D], F32R, r_bsp1 + 2 * KB)
        b0_lo = place("b0_lo", [P, D], F32R, r_bsp1 + 4 * KB)
        gh = [place(f"gh{h}", [P, TT, ER0], F32, r_asp + 2 * h * KB) for h in range(NH)]

        act_hi = place("act_hi", [P, FT * TOKENS], F32R, r_act)
        act_lo = place("act_lo", [P, FT * TOKENS], F32R, r_act + FT * TOKENS * 4)
        x1_hi = place("x1_hi", [P, KT, TOKENS], F32R, r_x1)
        x1_lo = place("x1_lo", [P, KT, TOKENS], F32R, r_x1 + 16 * KB)
        w_raw = [place(f"w_raw{s}", [P, 2 * KT * P], F32, r_wraw + 4 * KB * s) for s in range(2)]
        w_hi = [place(f"w_hi{s}", [P, 2, KT, P], F32R, r_wsp + 8 * KB * s) for s in range(2)]
        w_lo = [place(f"w_lo{s}", [P, 2, KT, P], F32R, r_wsp + 8 * KB * s + 4 * KB) for s in range(2)]
        g_raw = [place(f"g_raw{s}", [P, NG, GW], F32, r_graw + NG * GW * 4 * s) for s in range(2)]
        b_hi = [place(f"b_hi{s}", [P, NG, 2 * P], F32R, (r_bsp0, r_bsp1)[s]) for s in range(2)]
        b_lo = [place(f"b_lo{s}", [P, NG, 2 * P], F32R, (r_bsp0, r_bsp1)[s] + 4 * KB) for s in range(2)]
        ad_hi = [place(f"ad_hi{s}", [P, NG * P], F32R, r_asp + 4 * KB * s) for s in range(2)]
        ad_lo = [place(f"ad_lo{s}", [P, NG * P], F32R, r_asp + 4 * KB * s + 2 * KB) for s in range(2)]
        t_hi = place("t_hi", [P, 2, TOKENS], F32R, r_t)
        t_lo = place("t_lo", [P, 2, TOKENS], F32R, r_t + 8 * KB)
        silu = [place(f"silu{h}", [P, HALF], F32, r_misc + 2 * KB * h) for h in range(NH)]

        WD = FT * P * 4
        wd_raw = place("wd_raw", [P, FT * P], F32, r_wraw)
        wd_hi = [place(f"wd_hi{s}", [P, FT, P], F32R, (r_graw, r_wsp)[s]) for s in range(2)]
        wd_lo = [place(f"wd_lo{s}", [P, FT, P], F32R, (r_graw, r_wsp)[s] + WD) for s in range(2)]
        bd_raw = place("bd_raw", [P, NG, D], F32, r_bsp1)
        bd_hi = place("bd_hi", [P, NG, D], F32R, r_t)
        bd_lo = place("bd_lo", [P, NG, D], F32R, r_t + 8 * KB)
        td_hi = place("td_hi", [P, TOKENS], F32R, r_misc)
        td_lo = place("td_lo", [P, TOKENS], F32R, r_misc + 4 * KB)
        y_sb = place("y_sb", [P, KT, TOKENS], F32, r_bsp0)

        def small(name, shape, dt):
            n = 4
            for s in shape[1:]:
                n *= s
            return place(name, shape, dt, region(n))

        cst = small("cst", [P, C_END], F32)
        id_sb = small("id_sb", [P, NH * TT + NG], I32)
        idf = small("idf", [P, NH * TT + NG], F32)
        row_f = small("row_f", [P, 2, NG], F32)
        row_idx = small("row_idx", [P, FT * NG], I32)
        tile_idx = [small(f"tile_idx{s}", [P, NG], I32) for s in range(2)]
        lang_hot = small("lang_hot", [P, NH * TT, E0], F32)
        logits = small("logits", [P, TT, E0], F32)
        top8 = small("top8", [P, TT, 8], F32)
        top8_idx = small("top8_idx", [P, TT, 8], U32)
        top_f = small("top_f", [P, TT, 2], F32)
        margin = small("margin", [P, TT], F32)
        e_margin = small("e_margin", [P, TT], F32)
        wsum = small("wsum", [P, TT], F32)
        wtop = small("wtop", [P, 2, TT], F32)
        hot = small("hot", [P, 2, TT, E0], F32)
        gate = small("gate", [P, TT, E0], F32)
        assert cursor[0] <= nc.sbuf_usable_end, cursor[0]

        ps = ctx.enter_context(nc.psum_tensor("ps", [P, 8, HALF], F32))
        BANK_GHT, BANK_TURN, BANK_OUT = 2, 3, 4

        mask = cst[:, C_MASK:C_MASK + GT]
        ident = cst[:, C_ID:C_ID + P]
        iota8 = cst[:, C_IOTA:C_IOTA + E0]

        cst_landed = sem("cst_landed")
        id_landed = sem("id_landed")
        ar_landed = sem("ar_landed")
        x_landed = [[sem(f"x_landed{h}{k}") for k in range(KT)] for h in range(NH)]
        w0_landed = [sem(f"w0_landed{k}") for k in range(KT)]
        b0_landed = sem("b0_landed")
        a_landed = sem("a_landed")
        w_landed = [sem(f"w_landed{s}") for s in range(2)]
        g_landed = [sem(f"g_landed{s}") for s in range(2)]
        wd_landed = sem("wd_landed")
        bd_landed = sem("bd_landed")
        y_stored = sem("y_stored")

        idx_ready = sem("idx_ready")
        tile_idx_ready = sem("tile_idx_ready")
        small_step = sem("small_step")
        ar_hi_done, ar_lo_done = sem("ar_hi_done"), sem("ar_lo_done")
        x_hi_done, x_lo_done = sem("x_hi_done"), sem("x_lo_done")
        w0_hi_done, w0_lo_done = sem("w0_hi_done"), sem("w0_lo_done")
        b0_hi_done, b0_lo_done = sem("b0_hi_done"), sem("b0_lo_done")
        h_done = sem("h_done")
        margin_done = sem("margin_done")
        exp_done = sem("exp_done")
        gh_done = sem("gh_done")
        gh_turned, ghT_hi_done, ghT_lo_done = sem("gh_turned"), sem("ghT_hi_done"), sem("ghT_lo_done")
        a_turned, at_hi_done, at_lo_done = sem("a_turned"), sem("at_hi_done"), sem("at_lo_done")
        base0_done = sem("base0_done")
        out0_done = sem("out0_done")
        x1_added, x1_hi_done, x1_lo_done = sem("x1_added"), sem("x1_hi_done"), sem("x1_lo_done")
        t_done, t_masked, t_hi_done, t_lo_done = sem("t_done"), sem("t_masked"), sem("t_hi_done"), sem("t_lo_done")
        w_hi_done, w_lo_done = sem("w_hi_done"), sem("w_lo_done")
        b_hi_done, b_lo_done = sem("b_hi_done"), sem("b_lo_done")
        ad_turned, ad_hi_done, ad_lo_done = sem("ad_turned"), sem("ad_hi_done"), sem("ad_lo_done")
        gate_done, up_done = sem("gate_done"), sem("up_done")
        silu_done, glu_done = sem("silu_done"), sem("glu_done")
        act_hi_done, act_lo_done = sem("act_hi_done"), sem("act_lo_done")
        tdown_done, td_masked = sem("tdown_done"), sem("td_masked")
        td_hi_done, td_lo_done = sem("td_hi_done"), sem("td_lo_done")
        wd_hi_done, wd_lo_done = sem("wd_hi_done"), sem("wd_lo_done")
        bd_hi_done, bd_lo_done = sem("bd_hi_done"), sem("bd_lo_done")
        down_done = sem("down_done")
        x1f_done = sem("x1f_done")
        y_done = sem("y_done")

        def group_tokens(g):
            return slice(g * GT, (g + 1) * GT)

        block = ctx.enter_context(nc.Block())

        @block.sync
        def _(sp):
            sp.dma_start(ar_raw[:], ar0T).then_inc(ar_landed, 16)
            for k in range(KT):
                sp.dma_start(x_raw[0][:, k, :], xT[0, k]).then_inc(x_landed[0][k], 16)
            for k in range(KT):
                sp.dma_start(w0_raw[:, k, :], w0T[k]).then_inc(w0_landed[k], 16)
            sp.dma_start(b0_raw[:], b0T).then_inc(b0_landed, 16)
            for k in range(KT):
                sp.dma_start(x_raw[1][:, k, :], xT[1, k]).then_inc(x_landed[1][k], 16)

            def load_gate_up(i, u):
                sp.dma_start(w_raw[u][:], wgu[2 * i + u]).then_inc(w_landed[u], 16)

            load_gate_up(0, 0)
            load_gate_up(0, 1)
            with sp.Fori(1, FT // 2) as i:
                for u in range(2):
                    sp.wait_ge(w_lo_done, 2 * i + u - 1)
                    load_gate_up(i, u)
            sp.wait_ge(w_lo_done, FT - 2)
            load_gate_up(FT // 2, 0)

            sp.wait_ge(w_lo_done, FT)
            for m in range(KT):
                if m:
                    sp.wait_ge(wd_lo_done, m)
                sp.dma_start(wd_raw[:], wd[m]).then_inc(wd_landed, 16)
                if m >= 2:
                    for h in range(NH):
                        sp.wait_ge(y_done, NH * (m - 2) + h + 1)
                        sp.dma_start(out[m - 2, h], y_sb[:, m - 2, h * HALF:(h + 1) * HALF]).then_inc(y_stored, 16)
            for m in range(KT - 2, KT):
                for h in range(NH):
                    sp.wait_ge(y_done, NH * m + h + 1)
                    sp.dma_start(out[m, h], y_sb[:, m, h * HALF:(h + 1) * HALF]).then_inc(y_stored, 16)
            sp.wait_ge(y_stored, 16 * KT * NH)

        @block.gpsimd
        def _(pool):
            def gather(dst, table, index, landed):
                pool.indirect_dma_start(out=dst, out_offset=None, in_=table,
                                        in_offset=bass.IndirectOffsetOnAxis(ap=index, axis=0)).then_inc(landed, 16)

            for k in range(KT):
                pool.wait_ge(w0_hi_done, k + 1)
                nc.gpsimd.tensor_tensor(w0_lo[:, k, :], w0_raw[:, k, :], w0_hi[:, k, :].bitcast(F32),
                                        ALU.subtract).then_inc(w0_lo_done, 1)
                if k == 0:
                    pool.wait_ge(idx_ready, 1)
                    for g in range(NG):
                        gather(a_raw[:, g, :], a_rows, row_idx[:, g:g + 1], a_landed)
            pool.wait_ge(b0_hi_done, 1)
            nc.gpsimd.tensor_tensor(b0_lo[:], b0_raw[:], b0_hi[:].bitcast(F32),
                                    ALU.subtract).then_inc(b0_lo_done, 1)

            def gather_tile(i, u):
                f = 2 * i + u
                nc.gpsimd.tensor_copy(tile_idx[u][:], row_idx[:, bass.ds(f * NG, NG)]).then_inc(tile_idx_ready, 1)
                pool.wait_ge(tile_idx_ready, f + 1)
                pool.nop(nofuse=True)
                for g in range(NG):
                    gather(g_raw[u][:, g, :], ft_rows, tile_idx[u][:, g:g + 1], g_landed[u])

            pool.wait_ge(x_landed[1][KT - 1], 16)
            gather_tile(0, 0)
            gather_tile(0, 1)
            with pool.Fori(1, FT // 2) as i:
                for u in range(2):
                    pool.wait_ge(b_lo_done, 2 * i + u - 1)
                    pool.wait_ge(ad_turned, 2 * i + u - 1)
                    gather_tile(i, u)
            pool.wait_ge(b_lo_done, FT - 2)
            pool.wait_ge(ad_turned, FT - 2)
            gather_tile(FT // 2, 0)

            pool.wait_ge(up_done, HSTEPS - 2)
            for g in range(NG):
                gather(bd_raw[:, g, :], bd_rows, row_idx[:, g:g + 1], bd_landed)
            pool.wait_ge(up_done, HSTEPS)
            pool.wait_ge(tdown_done, FT)
            for m in range(KT):
                for h in range(NH):
                    part = slice(h * HALF, (h + 1) * HALF)
                    nc.gpsimd.tensor_tensor(y_sb[:, m, part], x1_hi[:, m, part].bitcast(F32),
                                            x1_lo[:, m, part].bitcast(F32), ALU.add).then_inc(x1f_done, 1)

        @block.scalar
        def _(act):
            def copy_hi(dst, src, done):
                nc.scalar.activation(dst, src, ACT.Copy).then_inc(done, 1)

            act.dma_start(id_sb[:], ids).then_inc(id_landed, 16)
            act.dma_start(cst[:], consts).then_inc(cst_landed, 16)

            act.wait_ge(ar_landed, 16)
            copy_hi(ar_hi[:], ar_raw[:], ar_hi_done)
            for k in range(KT):
                act.wait_ge(x_landed[0][k], 16)
                copy_hi(x_hi[0][:, k, :], x_raw[0][:, k, :], x_hi_done)
            for k in range(KT):
                act.wait_ge(w0_landed[k], 16)
                copy_hi(w0_hi[:, k, :], w0_raw[:, k, :], w0_hi_done)

            def exp_margin(h):
                act.wait_ge(margin_done, h + 1)
                nc.scalar.activation(e_margin[:], margin[:], ACT.Exp).then_inc(exp_done, 1)

            def turned_a_hi(j):
                act.wait_ge(a_turned, j + 1)
                if j == 0:
                    act.wait_ge(w0_lo_done, KT)
                copy_hi(at_hi[j // 4][:, j // 2 % 2, j % 2, :], ps[:, BANK_TURN, :], at_hi_done)

            def turned_gh_hi(h):
                act.wait_ge(gh_turned, h + 1)
                copy_hi(ghT_hi[:, h * HALF:(h + 1) * HALF], ps[:, BANK_GHT, :], ghT_hi_done)

            def x1_hi_part(h):
                for m in range(KT):
                    act.wait_ge(x1_added, KT * h + m + 1)
                    copy_hi(x1_hi[:, m, h * HALF:(h + 1) * HALF], ps[:, BANK_OUT + m, :], x1_hi_done)

            exp_margin(0)
            act.wait_ge(b0_landed, 16)
            copy_hi(b0_hi[:], b0_raw[:], b0_hi_done)
            turned_a_hi(0)
            for k in range(KT):
                act.wait_ge(x_landed[1][k], 16)
                copy_hi(x_hi[1][:, k, :], x_raw[1][:, k, :], x_hi_done)
            turned_a_hi(1)
            turned_gh_hi(0)
            turned_a_hi(2)
            turned_a_hi(3)
            x1_hi_part(0)
            exp_margin(1)
            turned_a_hi(4)
            turned_a_hi(5)
            turned_gh_hi(1)
            turned_a_hi(6)
            turned_a_hi(7)
            x1_hi_part(1)

            def split_tile(i, u, used):
                act.wait_ge(w_landed[u], 16 * (i + 1))
                if used is not None:
                    act.wait_ge(up_done, used)
                copy_hi(w_hi[u][:].rearrange("p a k f -> p (a k f)"), w_raw[u][:], w_hi_done)
                act.wait_ge(g_landed[u], 16 * NG * (i + 1))
                copy_hi(b_hi[u][:], g_raw[u][:, :, 0:2 * P], b_hi_done)

            act.wait_ge(w_landed[0], 16)
            split_tile(0, 0, None)

            for h in range(NH):
                for mat in range(2):
                    act.wait_ge(t_masked, 2 * h + mat + 1)
                    copy_hi(t_hi[:, mat, h * HALF:(h + 1) * HALF], ps[:, 2 * h + mat, :], t_hi_done)

            def glu(i, u, h, first=False):
                step = 2 * (2 * i + u) + h
                act.wait_ge(gate_done, step + 1)
                if not first:
                    act.wait_ge(glu_done, step - 1)
                nc.scalar.activation(silu[h][:], ps[:, 4 + 2 * h, :], ACT.Silu).then_inc(silu_done, 1)
                act.wait_ge(glu_done, step + 1)
                copy_hi(act_hi[:, bass.ds(step * HALF, HALF)], ps[:, 5 + 2 * h, :], act_hi_done)

            def turned_ad_hi(i, u, first=False):
                f = 2 * i + u
                act.wait_ge(ad_turned, f + 1)
                if not first:
                    act.wait_ge(tdown_done, f - 1)
                copy_hi(ad_hi[u][:], ps[:, 2, :], ad_hi_done)

            def tile_work(i, u, first=False):
                split_tile(i + u, 1 - u, None if first and u == 0 else 2 * (2 * i + u))
                glu(i, u, 0, first)
                turned_ad_hi(i, u, first)
                glu(i, u, 1, first)

            tile_work(0, 0, True)
            split_tile(1, 0, 2)
            glu(0, 1, 0)
            turned_ad_hi(0, 1, True)
            glu(0, 1, 1)
            with act.Fori(1, FT // 2) as i:
                for u in range(2):
                    tile_work(i, u)
            glu(FT // 2, 0, 0)
            turned_ad_hi(FT // 2, 0)

            def down_hi(m):
                act.wait_ge(wd_landed, 16 * (m + 1))
                if m == 0:
                    act.wait_ge(b_lo_done, FT)
                    act.wait_ge(ad_turned, FT)
                elif m == 1:
                    act.wait_ge(up_done, HSTEPS)
                else:
                    act.wait_ge(down_done, NH * (m - 1))
                copy_hi(wd_hi[m % 2][:].rearrange("p f n -> p (f n)"), wd_raw[:], wd_hi_done)

            down_hi(0)
            glu(FT // 2, 0, 1)
            act.wait_ge(bd_landed, 16 * NG)
            act.wait_ge(up_done, HSTEPS)
            copy_hi(bd_hi[:], bd_raw[:], bd_hi_done)
            for h in range(NH):
                act.wait_ge(td_masked, h + 1)
                copy_hi(td_hi[:, h * HALF:(h + 1) * HALF], ps[:, h, :], td_hi_done)
            for m in range(1, KT):
                down_hi(m)

        @block.vector
        def _(dve):
            chain = [0]

            def link(ins):
                chain[0] += 1
                ins.then_inc(small_step, 1)
                dve.wait_ge(small_step, chain[0])

            def sub_lo(dst, src, hi, done):
                nc.vector.tensor_tensor(dst, src, hi.bitcast(F32), ALU.subtract).then_inc(done, 1)

            dve.wait_ge(id_landed, 16)
            link(nc.vector.tensor_copy(idf[:], id_sb[:]))
            e_of = idf[:, NH * TT:]
            link(nc.vector.tensor_scalar(row_f[:, 0, :], e_of, 0.0, float(E1), ALU.is_lt, ALU.mult))
            link(nc.vector.tensor_tensor(row_f[:, 1, :], row_f[:, 0, :], e_of, ALU.add))
            link(nc.vector.tensor_scalar(row_f[:, 0, :], row_f[:, 1, :], 0.0, float(E1 - 1), ALU.max, ALU.min))
            dve.wait_ge(cst_landed, 16)
            link(nc.vector.tensor_scalar(row_f[:, 1, :], row_f[:, 0, :], float(R1), cst[:, C_ROFF:C_ROFF + 1],
                                         ALU.mult, ALU.add))
            nc.vector.tensor_tensor(row_idx[:].rearrange("p (f g) -> p f g", g=NG),
                                    cst[:, C_FTOFF:C_FTOFF + FT * NG].rearrange("p (f g) -> p f g", g=NG),
                                    row_f[:, 1, :].unsqueeze(1).to_broadcast([P, FT, NG]),
                                    ALU.add).then_inc(idx_ready, 1)
            link(nc.vector.tensor_tensor(lang_hot[:], iota8.unsqueeze(1).to_broadcast([P, NH * TT, E0]),
                                         idf[:, 0:NH * TT].unsqueeze(2).to_broadcast([P, NH * TT, E0]),
                                         ALU.is_equal))

            dve.wait_ge(ar_hi_done, 1)
            sub_lo(ar_lo[:], ar_raw[:], ar_hi[:], ar_lo_done)

            def x_lo_part(h):
                for k in range(KT):
                    dve.wait_ge(x_hi_done, KT * h + k + 1)
                    sub_lo(x_lo[h][:, k, :], x_raw[h][:, k, :], x_hi[h][:, k, :], x_lo_done)

            def gating(h):
                ps_h = ps[:, 0:2, 0:2 * HC].rearrange("p b (t c) -> p b t c", c=HC)
                dve.wait_ge(h_done, h + 1)
                for b in range(2):
                    last = nc.vector.scalar_tensor_tensor(
                        out=logits[:, 2 * b:2 * b + 2, :], in0=lang_hot[:, TT * h + 2 * b:TT * h + 2 * b + 2, :],
                        scalar=LANG_BIAS, in1=ps_h[:, b, :, ER0:HC], op0=ALU.mult, op1=ALU.add)
                link(last)
                for t in range(TT):
                    last = nc.vector.max(top8[:, t, :], logits[:, t, :])
                link(last)
                if h:
                    dve.wait_ge(exp_done, h)
                nc.vector.tensor_tensor(margin[:], top8[:, :, 1], top8[:, :, 0],
                                        ALU.subtract).then_inc(margin_done, 1)
                for t in range(TT):
                    last = nc.vector.max_index(top8_idx[:, t, :], top8[:, t, :], logits[:, t, :])
                link(last)
                link(nc.vector.tensor_copy(top_f[:], top8_idx[:, :, 0:2]))
                for j in range(2):
                    last = nc.vector.tensor_tensor(
                        hot[:, j], iota8.unsqueeze(1).to_broadcast([P, TT, E0]),
                        top_f[:, :, j:j + 1].to_broadcast([P, TT, E0]), ALU.is_equal)
                link(last)
                dve.wait_ge(exp_done, h + 1)
                link(nc.vector.tensor_scalar(wsum[:], e_margin[:], 1.0, None, ALU.add))
                link(nc.vector.reciprocal(wtop[:, 1, :], wsum[:]))
                link(nc.vector.tensor_scalar(wtop[:, 0, :], wtop[:, 1, :], SCALING, None, ALU.mult))
                link(nc.vector.tensor_tensor(wtop[:, 1, :], e_margin[:], wtop[:, 0, :], ALU.mult))
                link(nc.vector.tensor_tensor(hot[:], hot[:], wtop[:].unsqueeze(3).to_broadcast([P, 2, TT, E0]),
                                             ALU.mult))
                link(nc.vector.tensor_tensor(gate[:], hot[:, 0], hot[:, 1], ALU.add))
                for b in range(2):
                    last = nc.vector.tensor_tensor(
                        gh[h][:, 2 * b:2 * b + 2, :].rearrange("p t (e r) -> p t e r", r=R0),
                        ps_h[:, b, :, 0:ER0].rearrange("p t (e r) -> p t e r", r=R0),
                        gate[:, 2 * b:2 * b + 2, :].unsqueeze(3).to_broadcast([P, 2, E0, R0]), ALU.mult)
                last.then_inc(gh_done, 1)
                dve.wait_ge(gh_done, h + 1)

            def turned_a_lo(j):
                dve.wait_ge(at_hi_done, j + 1)
                at = (slice(None), j // 2 % 2, j % 2, slice(None))
                sub_lo(at_lo[j // 4][at], ps[:, BANK_TURN, :], at_hi[j // 4][at], at_lo_done)

            def turned_gh_lo(h):
                part = slice(h * HALF, (h + 1) * HALF)
                dve.wait_ge(ghT_hi_done, h + 1)
                sub_lo(ghT_lo[:, part], ps[:, BANK_GHT, :], ghT_hi[:, part], ghT_lo_done)

            def x1_part(h):
                def add(m):
                    dve.wait_ge(out0_done, KT * h + m + 1)
                    nc.vector.tensor_tensor(ps[:, BANK_OUT + m, :], ps[:, BANK_OUT + m, :], x_raw[h][:, m, :],
                                            ALU.add).then_inc(x1_added, 1)

                def lo(m):
                    part = (slice(None), m, slice(h * HALF, (h + 1) * HALF))
                    dve.wait_ge(x1_hi_done, KT * h + m + 1)
                    sub_lo(x1_lo[part], ps[:, BANK_OUT + m, :], x1_hi[part], x1_lo_done)

                add(0)
                for m in range(1, KT):
                    add(m)
                    lo(m - 1)
                lo(KT - 1)

            x_lo_part(0)
            gating(0)
            turned_a_lo(0)
            x_lo_part(1)
            turned_a_lo(1)
            turned_gh_lo(0)
            turned_a_lo(2)
            turned_a_lo(3)
            x1_part(0)
            gating(1)
            turned_a_lo(4)
            turned_a_lo(5)
            turned_gh_lo(1)
            turned_a_lo(6)
            turned_a_lo(7)
            x1_part(1)

            def split_tile(i, u):
                f = 2 * i + u
                dve.wait_ge(w_hi_done, f + 1)
                sub_lo(w_lo[u][:].rearrange("p a k f -> p (a k f)"), w_raw[u][:],
                       w_hi[u][:].rearrange("p a k f -> p (a k f)"), w_lo_done)
                dve.wait_ge(b_hi_done, f + 1)
                sub_lo(b_lo[u][:], g_raw[u][:, :, 0:2 * P], b_hi[u][:], b_lo_done)

            def mask_blocks(bank, done):
                v = ps[:, bank, :].rearrange("p (g t) -> p g t", g=GH)
                nc.vector.tensor_tensor(v, v, mask.unsqueeze(1).to_broadcast([P, GH, GT]),
                                        ALU.mult).then_inc(done, 1)

            split_tile(0, 0)
            for h in range(NH):
                for mat in range(2):
                    dve.wait_ge(t_done, 2 * h + mat + 1)
                    mask_blocks(2 * h + mat, t_masked)
                for mat in range(2):
                    part = (slice(None), mat, slice(h * HALF, (h + 1) * HALF))
                    dve.wait_ge(t_hi_done, 2 * h + mat + 1)
                    sub_lo(t_lo[part], ps[:, 2 * h + mat, :], t_hi[part], t_lo_done)

            def glu(i, u, h):
                step = 2 * (2 * i + u) + h
                part = bass.ds(step * HALF, HALF)
                dve.wait_ge(silu_done, step + 1)
                dve.wait_ge(up_done, step + 1)
                nc.vector.tensor_tensor(ps[:, 5 + 2 * h, :], ps[:, 5 + 2 * h, :], silu[h][:],
                                        ALU.mult).then_inc(glu_done, 1)
                dve.wait_ge(act_hi_done, step + 1)
                sub_lo(act_lo[:, part], ps[:, 5 + 2 * h, :], act_hi[:, part], act_lo_done)

            def turned_ad_lo(i, u):
                dve.wait_ge(ad_hi_done, 2 * i + u + 1)
                sub_lo(ad_lo[u][:], ps[:, 2, :], ad_hi[u][:], ad_lo_done)

            def tile_work(i, u):
                split_tile(i + u, 1 - u)
                glu(i, u, 0)
                turned_ad_lo(i, u)
                glu(i, u, 1)

            tile_work(0, 0)
            tile_work(0, 1)
            with dve.Fori(1, FT // 2) as i:
                for u in range(2):
                    tile_work(i, u)
            glu(FT // 2, 0, 0)
            turned_ad_lo(FT // 2, 0)

            def down_lo(m):
                dve.wait_ge(wd_hi_done, m + 1)
                sub_lo(wd_lo[m % 2][:].rearrange("p f n -> p (f n)"), wd_raw[:],
                       wd_hi[m % 2][:].rearrange("p f n -> p (f n)"), wd_lo_done)

            down_lo(0)
            glu(FT // 2, 0, 1)
            dve.wait_ge(bd_hi_done, 1)
            sub_lo(bd_lo[:], bd_raw[:], bd_hi[:], bd_lo_done)
            for h in range(NH):
                dve.wait_ge(tdown_done, FT)
                mask_blocks(h, td_masked)
            for h in range(NH):
                part = slice(h * HALF, (h + 1) * HALF)
                dve.wait_ge(td_hi_done, h + 1)
                sub_lo(td_lo[:, part], ps[:, h, :], td_hi[:, part], td_lo_done)
            down_lo(1)
            for m in range(KT):
                for h in range(NH):
                    part = slice(h * HALF, (h + 1) * HALF)
                    dve.wait_ge(down_done, NH * m + h + 1)
                    dve.wait_ge(x1f_done, NH * m + h + 1)
                    nc.vector.tensor_tensor(y_sb[:, m, part], ps[:, BANK_OUT + 2 * (m % 2) + h, :],
                                            y_sb[:, m, part], ALU.add).then_inc(y_done, 1)
                if m + 2 < KT:
                    down_lo(m + 2)

        @block.tensor
        def _(pe):
            def three_passes(o, a_hi, a_lo, m_hi, m_lo, start=False, stop=False, shared=False):
                pe.matmul(o, a_hi, m_hi, start=start, stop=False, skip_group_check=shared)
                pe.matmul(o, a_hi, m_lo, start=False, stop=False, skip_group_check=shared)
                return pe.matmul(o, a_lo, m_hi, start=False, stop=stop, skip_group_check=shared)

            def lora_a_and_router(h):
                pe.wait_ge(ar_lo_done, 1)
                if h:
                    pe.wait_ge(gh_done, h)
                for k in range(KT):
                    pe.wait_ge(x_lo_done, KT * h + k + 1)
                    for t in range(TT):
                        tok = slice(t * P, (t + 1) * P)
                        last = three_passes(ps[:, t // 2, (t % 2) * HC:(t % 2 + 1) * HC],
                                            x_hi[h][:, k, tok], x_lo[h][:, k, tok], ar_hi[:, k, :], ar_lo[:, k, :],
                                            start=(k == 0 and t % 2 == 0), stop=(k == KT - 1), shared=True)
                last.then_inc(h_done, 1)

            def turn_a(j):
                if j == 0:
                    pe.wait_ge(a_landed, 16 * NG)
                    pe.wait_ge(cst_landed, 16)
                if j:
                    pe.wait_ge(at_lo_done, j)
                for k in range(KT):
                    col = (j % 2) * D + k * P
                    last = pe.transpose(ps[:, BANK_TURN, k * P:(k + 1) * P], a_raw[:, j // 2, col:col + P], ident)
                last.then_inc(a_turned, 1)

            def turn_gh(h):
                pe.wait_ge(cst_landed, 16)
                pe.wait_ge(gh_done, h + 1)
                if h:
                    pe.wait_ge(ghT_lo_done, h)
                for t in range(TT):
                    last = pe.transpose(ps[:, BANK_GHT, t * P:(t + 1) * P], gh[h][:, t, :], ident)
                last.then_inc(gh_turned, 1)

            def base0(h):
                for k in range(KT):
                    pe.wait_ge(w0_lo_done, k + 1)
                    for m in range(KT):
                        if h and k == 0:
                            pe.wait_ge(x1_lo_done, m + 1)
                        last = three_passes(ps[:, BANK_OUT + m, :], w0_hi[:, k, m * P:(m + 1) * P],
                                            w0_lo[:, k, m * P:(m + 1) * P], x_hi[h][:, k, :], x_lo[h][:, k, :],
                                            start=(k == 0))
                    if k == KT - 1:
                        last.then_inc(base0_done, 1)
                    if k == 2:
                        turn_gh(h)
                    turn_a(KT * h + k)

            def lora0(h):
                pe.wait_ge(ghT_lo_done, h + 1)
                pe.wait_ge(b0_lo_done, 1)
                part = slice(h * HALF, (h + 1) * HALF)
                for m in range(KT):
                    three_passes(ps[:, BANK_OUT + m, :], b0_hi[:, m * P:(m + 1) * P], b0_lo[:, m * P:(m + 1) * P],
                                 ghT_hi[:, part], ghT_lo[:, part], stop=True).then_inc(out0_done, 1)

            for h in range(NH):
                lora_a_and_router(h)
                base0(h)
                lora0(h)

            def lora_t(h):
                pe.wait_ge(x1_lo_done, KT * (h + 1))
                pe.wait_ge(at_lo_done, 4 * (h + 1))
                if h == 0:
                    pe.wait_ge(gh_done, NH)
                else:
                    pe.wait_ge(ghT_lo_done, NH)
                    pe.wait_ge(at_lo_done, 4 * NH)
                for mat in range(2):
                    for gl in range(GH):
                        for k in range(KT):
                            a = (slice(None), gl, mat, slice(k * P, (k + 1) * P))
                            tok = group_tokens(h * GH + gl)
                            last = three_passes(ps[:, 2 * h + mat, gl * GT:(gl + 1) * GT], at_hi[h][a], at_lo[h][a],
                                                x1_hi[:, k, tok], x1_lo[:, k, tok],
                                                start=(k == 0), stop=(k == KT - 1))
                    last.then_inc(t_done, 1)

            lora_t(0)
            lora_t(1)

            def gate_up(i, u, h, first=False):
                step = 2 * (2 * i + u) + h
                if h == 0:
                    pe.wait_ge(w_lo_done, 2 * i + u + 1)
                half = slice(h * HALF, (h + 1) * HALF)
                for mat, (done, freed) in enumerate(((gate_done, silu_done), (up_done, act_lo_done))):
                    if not first:
                        pe.wait_ge(freed, step - 1)
                    bank = 4 + 2 * h + mat
                    for k in range(KT):
                        three_passes(ps[:, bank, :], w_hi[u][:, mat, k, :], w_lo[u][:, mat, k, :],
                                     x1_hi[:, k, half], x1_lo[:, k, half], start=(k == 0))
                    if mat == 0:
                        pe.wait_ge(b_lo_done, 2 * i + u + 1)
                        if first:
                            pe.wait_ge(t_lo_done, 2 * h + 2)
                    for gl in range(GH):
                        g = h * GH + gl
                        b = (slice(None), g, slice(mat * P, (mat + 1) * P))
                        last = three_passes(ps[:, bank, gl * GT:(gl + 1) * GT], b_hi[u][b], b_lo[u][b],
                                            t_hi[:, mat, group_tokens(g)], t_lo[:, mat, group_tokens(g)],
                                            stop=(gl == GH - 1))
                    last.then_inc(done, 1)

            def turn_a_down(i, u, first=False):
                pe.wait_ge(g_landed[u], 16 * NG * (i + 1))
                if first:
                    pe.wait_ge(t_lo_done, 2 * NH)
                else:
                    pe.wait_ge(ad_lo_done, 2 * i + u)
                for g in range(NG):
                    last = pe.transpose(ps[:, 2, g * P:(g + 1) * P], g_raw[u][:, g, 2 * P:3 * P], ident)
                last.then_inc(ad_turned, 1)

            def lora_t_down(i, u, first=False, last_tile=False):
                f = 2 * i + u
                rows = F_LAST if last_tile else P
                pe.wait_ge(ad_lo_done, f + 1)
                pe.wait_ge(act_lo_done, 2 * f + 2)
                for g in range(NG):
                    at = bass.ds(f * TOKENS + g * GT, GT)
                    last = three_passes(ps[:, g // GH, (g % GH) * GT:(g % GH + 1) * GT],
                                        ad_hi[u][0:rows, g * P:(g + 1) * P], ad_lo[u][0:rows, g * P:(g + 1) * P],
                                        act_hi[0:rows, at], act_lo[0:rows, at],
                                        start=(first and g % GH == 0), stop=last_tile, shared=True)
                last.then_inc(tdown_done, 1)

            gate_up(0, 0, 0, True)
            turn_a_down(0, 0, True)
            gate_up(0, 0, 1, True)
            gate_up(0, 1, 0)
            turn_a_down(0, 1)
            lora_t_down(0, 0, first=True)
            gate_up(0, 1, 1)
            with pe.Fori(1, FT // 2) as i:
                for u in range(2):
                    gate_up(i, u, 0)
                    turn_a_down(i, u)
                    lora_t_down(i + u - 1, 1 - u)
                    gate_up(i, u, 1)
            gate_up(FT // 2, 0, 0)
            turn_a_down(FT // 2, 0)
            lora_t_down(FT // 2 - 1, 1)
            gate_up(FT // 2, 0, 1)

            def down_base(m, h):
                bank = BANK_OUT + 2 * (m % 2) + h
                if m < 2:
                    pe.wait_ge(silu_done, HSTEPS - 1 + m)
                    pe.wait_ge(act_lo_done, HSTEPS - 1 + m)
                else:
                    pe.wait_ge(y_done, NH * (m - 2) + h + 1)
                pe.wait_ge(wd_lo_done, m + 1)
                for f in range(FT):
                    rows = F_LAST if f == FT - 1 else P
                    if m == 0 and f == FT - 1:
                        pe.wait_ge(act_lo_done, HSTEPS - 1 + h)
                    at = slice(f * TOKENS + h * HALF, f * TOKENS + (h + 1) * HALF)
                    three_passes(ps[:, bank, :], wd_hi[m % 2][0:rows, f, :], wd_lo[m % 2][0:rows, f, :],
                                 act_hi[0:rows, at], act_lo[0:rows, at], start=(f == 0))

            def down_lora(m, h):
                bank = BANK_OUT + 2 * (m % 2) + h
                pe.wait_ge(td_lo_done, NH)
                pe.wait_ge(bd_lo_done, 1)
                for gl in range(GH):
                    g = h * GH + gl
                    b = (slice(None), g, slice(m * P, (m + 1) * P))
                    last = three_passes(ps[:, bank, gl * GT:(gl + 1) * GT], bd_hi[b], bd_lo[b],
                                        td_hi[:, group_tokens(g)], td_lo[:, group_tokens(g)], stop=(gl == GH - 1))
                last.then_inc(down_done, 1)

            down_base(0, 0)
            lora_t_down(FT // 2, 0, last_tile=True)
            down_base(0, 1)
            for h in range(NH):
                down_lora(0, h)
            for m in range(1, KT):
                for h in range(NH):
                    down_base(m, h)
                    down_lora(m, h)


def kernel(**inputs):
    import numpy as np
    import concourse.bacc as bacc
    from concourse.bass_utils import run_bass_kernel_spmd

    a = {k: np.asarray(v) for k, v in inputs.items()}
    c = np.ascontiguousarray

    def f_tiles(w):
        order = np.concatenate([np.arange((FT - 1) * P, F), np.arange(F - P, F - F_LAST)])
        return np.stack([w[..., f * P:(f + 1) * P] for f in range(FT - 1)] + [w[..., order]], axis=-2)

    xT = c(a["x"].reshape(NH, HALF, KT, P).transpose(0, 2, 3, 1))
    w0T = c(a["L0_cond_W"].T.reshape(KT, P, D))
    ar = np.concatenate([a["L0_cond_A"].reshape(ER0, D), a["L0_cond_Wr"]], axis=0)
    ar0T = c(ar.T.reshape(KT, P, HC).transpose(1, 0, 2))
    b0T = c(a["L0_cond_B"].transpose(0, 2, 1).reshape(ER0, D))

    consts = np.zeros((P, C_END), np.float32)
    block = np.arange(P)[:, None] // R1 == np.arange(GT)[None, :] // BATCH_TOKENS
    consts[:, C_MASK:C_MASK + GT] = np.where(block, 0.5, 0.0)
    consts[:, C_ID:C_ID + P] = np.eye(P)
    consts[:, C_IOTA:C_IOTA + E0] = np.arange(E0)
    consts[:, C_FTOFF:C_FTOFF + FT * NG] = np.repeat(np.arange(FT) * E1 * R1, NG)
    consts[:, C_ROFF] = np.arange(P) % R1

    lang = np.repeat(a["itok_B_0_7"], BATCH_TOKENS).reshape(NH * TT, P).T
    expert = np.repeat(a["itok_B_2_6"], R1).reshape(NG, P).T
    ids = c(np.concatenate([lang, expert], axis=1))

    gu = np.stack([f_tiles(a["L1_cond_W_gate"].T), f_tiles(a["L1_cond_W_up"].T)])
    wgu = c(gu.reshape(2, KT, P, FT, P).transpose(3, 2, 0, 1, 4).reshape(FT, P, 2 * KT * P))
    a_rows = c(np.concatenate([a["L1_cond_A_gate"].reshape(E1 * R1, D), a["L1_cond_A_up"].reshape(E1 * R1, D)], axis=1))
    parts = [f_tiles(a[n][0].transpose(0, 2, 1).reshape(E1 * R1, F)) for n in ("L1_cond_B_gate", "L1_cond_B_up")]
    parts.append(f_tiles(a["L1_cond_A_down"][0].reshape(E1 * R1, F)))
    ft_rows = c(np.stack(parts, axis=2).transpose(1, 0, 2, 3).reshape(FT * E1 * R1, GW))
    wd = c(f_tiles(a["L1_cond_W_down"]).reshape(KT, P, FT, P).transpose(0, 3, 2, 1).reshape(KT, P, FT * P))
    bd_rows = c(a["L1_cond_B_down"][0].transpose(0, 2, 1).reshape(E1 * R1, D))

    arrays = {"in_xT": xT, "in_w0T": w0T, "in_ar0T": ar0T, "in_b0T": b0T, "in_consts": consts, "in_ids": ids,
              "in_wgu": wgu, "in_a_rows": a_rows, "in_ft_rows": ft_rows, "in_wd": wd, "in_bd_rows": bd_rows}
    nc = bacc.Bacc("TRN2", target_bir_lowering=False, num_devices=1)
    aps = [nc.dram_tensor(n, v.shape, mybir.dt.from_np(v.dtype), kind="ExternalInput").ap()
           for n, v in arrays.items()]
    out = nc.dram_tensor("out_yT", (KT, NH, P, HALF), F32, kind="ExternalOutput").ap()
    mlp_with_loras(nc, *aps, out)
    r = run_bass_kernel_spmd(nc, [arrays], core_ids=[0])
    y = r.results[0]["out_yT"]
    return c(y.transpose(1, 3, 0, 2)).reshape(a["x"].shape)
```

```python
from contextlib import ExitStack
from math import prod

import concourse.bass as bass
from concourse import mybir

ALU = mybir.AluOpType
ACT = mybir.ActivationFunctionType
F32 = mybir.dt.float32
F32R = mybir.dt.float32r
I32 = mybir.dt.int32
U32 = mybir.dt.uint32

P = 128
TOKENS = 1024
HALF = 512
NH = TOKENS // HALF
D = 512
KT = D // P
E0, R0 = 8, 16
ER0 = E0 * R0
HC = ER0 + E0
LANG_BIAS = 5.0
SCALING = 2.0
TT = HALF // P
E1, R1 = 16, 16
F = 1376
FT = -(-F // P)
F_LAST = F - (FT - 1) * P
BATCH_TOKENS = 32
GB = P // R1
GT = GB * BATCH_TOKENS
NG = TOKENS // GT
GH = NG // NH
HB = HALF // BATCH_TOKENS
AW = KT * 2 * R1
GW = 3 * P
HSTEPS = NH * FT

C_MASK, C_ID, C_IOTA, C_FTOFF, C_ROFF = 0, GT, GT + P, GT + P + E0, GT + P + E0 + FT * NG
C_END = C_ROFF + 1


def mlp_with_loras(nc, xT, w0T, ar0T, b0T, consts, ids, wgu, a_experts, ft_rows, wd, bd_rows, out):
    with ExitStack() as ctx:
        def sem(name):
            return ctx.enter_context(nc.semaphore(name))

        cursor = [-(-nc.sbuf_base // 32) * 32]

        def region(nbytes):
            at = cursor[0]
            cursor[0] += -(-nbytes // 32) * 32
            return at

        def place(name, shape, dt, at):
            return nc.alloc_sbuf_tensor_at(name, shape, dt, offset=at)

        KB = 1024
        r_act = region(FT * TOKENS * 8)
        r_x1 = region(KT * TOKENS * 8)
        r_wraw = region(8 * KB)
        r_graw = region(2 * NG * GW * 4)
        r_wsp = region(16 * KB)
        r_bsp1 = region(8 * KB)
        r_bsp0 = region(8 * KB)
        r_asp = region(8 * KB)
        r_t = region(16 * KB)
        r_misc = region(8 * KB)

        x_raw = [place(f"x_raw{h}", [P, KT, HALF], F32, r_act + h * 8 * KB) for h in range(NH)]
        x_hi = [place(f"x_hi{h}", [P, KT, HALF], F32R, r_act + (16 + 8 * h) * KB) for h in range(NH)]
        x_lo = [place(f"x_lo{h}", [P, KT, HALF], F32R, r_act + (32 + 8 * h) * KB) for h in range(NH)]
        w0_hi = place("w0_hi", [P, KT, D], F32R, r_act + 48 * KB)
        w0_lo = place("w0_lo", [P, KT, D], F32R, r_act + 56 * KB)
        w0_raw = place("w0_raw", [P, KT, D], F32, r_act + 64 * KB)
        ghT_hi = place("ghT_hi", [P, TOKENS], F32R, r_act + 72 * KB)
        ghT_lo = place("ghT_lo", [P, TOKENS], F32R, r_act + 76 * KB)
        AR = KT * HC * 4
        ar_raw = place("ar_raw", [P, KT, HC], F32, r_act + 80 * KB)
        ar_sp = place("ar_sp", [P, KT, 2, HC], F32R, r_act + 80 * KB + AR)
        at_shape = [P, GH, KT * 2, P]
        at_hi = [place("at_hi0", at_shape, F32R, r_act + 64 * KB), place("at_hi1", at_shape, F32R, r_act + 16 * KB)]
        at_lo = [place("at_lo0", at_shape, F32R, r_misc), place("at_lo1", at_shape, F32R, r_act + 32 * KB)]
        a_raw = place("a_raw", [P, NH * HB, AW], F32, r_t)
        b0_raw = place("b0_raw", [P, D], F32, r_bsp1)
        b0_hi = place("b0_hi", [P, D], F32R, r_bsp1 + 2 * KB)
        b0_lo = place("b0_lo", [P, D], F32R, r_bsp1 + 4 * KB)
        gh = [place(f"gh{h}", [P, TT, ER0], F32, r_asp + 2 * h * KB) for h in range(NH)]
        h_part = place("h_part", [P, TT, HC], F32, r_bsp0)
        h_sum = place("h_sum", [P, TT, HC], F32, r_bsp0 + TT * HC * 4)

        act_hi = place("act_hi", [P, FT * TOKENS], F32R, r_act)
        act_lo = place("act_lo", [P, FT * TOKENS], F32R, r_act + FT * TOKENS * 4)
        x1_hi = place("x1_hi", [P, KT, TOKENS], F32R, r_x1)
        x1_lo = place("x1_lo", [P, KT, TOKENS], F32R, r_x1 + 16 * KB)
        w_raw = [place(f"w_raw{s}", [P, 2 * KT * P], F32, r_wraw + 4 * KB * s) for s in range(2)]
        w_hi = [place(f"w_hi{s}", [P, 2, KT, P], F32R, r_wsp + 8 * KB * s) for s in range(2)]
        w_lo = [place(f"w_lo{s}", [P, 2, KT, P], F32R, r_wsp + 8 * KB * s + 4 * KB) for s in range(2)]
        g_raw = [place(f"g_raw{s}", [P, NG, GW], F32, r_graw + NG * GW * 4 * s) for s in range(2)]
        b_hi = [place(f"b_hi{s}", [P, NG, 2 * P], F32R, (r_bsp0, r_bsp1)[s]) for s in range(2)]
        b_lo = [place(f"b_lo{s}", [P, NG, 2 * P], F32R, (r_bsp0, r_bsp1)[s] + 4 * KB) for s in range(2)]
        ad_hi = [place(f"ad_hi{s}", [P, NG * P], F32R, r_asp + 4 * KB * s) for s in range(2)]
        ad_lo = [place(f"ad_lo{s}", [P, NG * P], F32R, r_asp + 4 * KB * s + 2 * KB) for s in range(2)]
        t_hi = place("t_hi", [P, 2, TOKENS], F32R, r_t)
        t_lo = place("t_lo", [P, 2, TOKENS], F32R, r_t + 8 * KB)
        silu = [place(f"silu{h}", [P, HALF], F32, r_misc + 2 * KB * h) for h in range(NH)]

        WD = FT * P * 4
        wd_raw = place("wd_raw", [P, FT * P], F32, r_wraw)
        wd_hi = [place(f"wd_hi{s}", [P, FT, P], F32R, (r_graw, r_wsp)[s]) for s in range(2)]
        wd_lo = [place(f"wd_lo{s}", [P, FT, P], F32R, (r_graw, r_wsp)[s] + WD) for s in range(2)]
        bd_raw = place("bd_raw", [P, NG, D], F32, r_bsp1)
        bd_hi = place("bd_hi", [P, NG, D], F32R, r_t)
        bd_lo = place("bd_lo", [P, NG, D], F32R, r_t + 8 * KB)
        td_hi = place("td_hi", [P, TOKENS], F32R, r_misc)
        td_lo = place("td_lo", [P, TOKENS], F32R, r_misc + 4 * KB)
        y_sb = place("y_sb", [P, KT, TOKENS], F32, r_bsp0)

        def small(name, shape, dt):
            return place(name, shape, dt, region(4 * prod(shape[1:])))

        cst = small("cst", [P, C_END], F32)
        NE = NG + NH * HB
        id_sb = small("id_sb", [P, NH * TT + NE], I32)
        idf = small("idf", [P, NH * TT + NE], F32)
        exp_f = small("exp_f", [P, 2, NE], F32)
        row_f = small("row_f", [P, NG], F32)
        batch_exp = small("batch_exp", [P, NH * HB], I32)
        row_idx = small("row_idx", [P, FT * NG], I32)
        tile_idx = [small(f"tile_idx{s}", [P, NG], I32) for s in range(2)]
        lang_hot = small("lang_hot", [P, NH * TT, E0], F32)
        scratch_at = [r_bsp0 + 2 * TT * HC * 4]

        def scratch(name, shape, dt):
            at = scratch_at[0]
            scratch_at[0] += -(-4 * prod(shape[1:]) // 32) * 32
            return place(name, shape, dt, at)

        logits = scratch("logits", [P, TT, E0], F32)
        top8 = scratch("top8", [P, TT, 8], F32)
        top8_idx = scratch("top8_idx", [P, TT, 8], U32)
        top_f = scratch("top_f", [P, TT, 2], F32)
        margin = scratch("margin", [P, TT], F32)
        e_margin = scratch("e_margin", [P, TT], F32)
        wsum = scratch("wsum", [P, TT], F32)
        wtop = scratch("wtop", [P, 2, TT], F32)
        hot = scratch("hot", [P, 2, TT, E0], F32)
        gate = scratch("gate", [P, TT, E0], F32)
        assert scratch_at[0] <= r_bsp0 + 8 * KB
        assert cursor[0] <= nc.sbuf_usable_end, cursor[0]

        ps = ctx.enter_context(nc.psum_tensor("ps", [P, 8, HALF], F32))
        BANK_GHT, BANK_OUT = 3, 4

        mask = cst[:, C_MASK:C_MASK + GT]
        ident = cst[:, C_ID:C_ID + P]
        iota8 = cst[:, C_IOTA:C_IOTA + E0]

        cst_landed = sem("cst_landed")
        id_landed = sem("id_landed")
        ar_landed = sem("ar_landed")
        x_landed = [[sem(f"x_landed{h}{k}") for k in range(KT)] for h in range(NH)]
        w0_landed = [sem(f"w0_landed{k}") for k in range(KT)]
        b0_landed = sem("b0_landed")
        a_landed = [sem(f"a_landed{h}") for h in range(NH)]
        w_landed = [sem(f"w_landed{s}") for s in range(2)]
        g_landed = [sem(f"g_landed{s}") for s in range(2)]
        wd_landed = sem("wd_landed")
        bd_landed = sem("bd_landed")
        y_stored = sem("y_stored")

        idx_ready = sem("idx_ready")
        batch_exp_ready = sem("batch_exp_ready")
        tile_idx_ready = sem("tile_idx_ready")
        small_step = sem("small_step")
        ar_hi_done, ar_lo_done = sem("ar_hi_done"), sem("ar_lo_done")
        x_hi_done, x_lo_done = sem("x_hi_done"), sem("x_lo_done")
        w0_hi0_done = sem("w0_hi0_done")
        w0_hi_done, w0_lo_done = sem("w0_hi_done"), sem("w0_lo_done")
        b0_hi_done, b0_lo_done = sem("b0_hi_done"), sem("b0_lo_done")
        h_done, h_copied, h_summed = sem("h_done"), sem("h_copied"), sem("h_summed")
        margin_done = sem("margin_done")
        exp_done = sem("exp_done")
        gh_done = sem("gh_done")
        gh_turned, ghT_hi_done, ghT_lo_done = sem("gh_turned"), sem("ghT_hi_done"), sem("ghT_lo_done")
        at_hi_done, at_lo_done = sem("at_hi_done"), sem("at_lo_done")
        base0_done = sem("base0_done")
        out0_done = sem("out0_done")
        x1_added, x1_hi_done, x1_lo_done = sem("x1_added"), sem("x1_hi_done"), sem("x1_lo_done")
        t_done, t_masked, t_hi_done, t_lo_done = sem("t_done"), sem("t_masked"), sem("t_hi_done"), sem("t_lo_done")
        w_hi_done, w_lo_done = sem("w_hi_done"), sem("w_lo_done")
        b_hi_done, b_lo_done = sem("b_hi_done"), sem("b_lo_done")
        ad_turned, ad_hi_done, ad_lo_done = sem("ad_turned"), sem("ad_hi_done"), sem("ad_lo_done")
        gate_done, up_done = sem("gate_done"), sem("up_done")
        silu_done, glu_done = sem("silu_done"), sem("glu_done")
        act_hi_done, act_lo_done = sem("act_hi_done"), sem("act_lo_done")
        tdown_done, td_masked = sem("tdown_done"), sem("td_masked")
        td_hi_done, td_lo_done = sem("td_hi_done"), sem("td_lo_done")
        wd_hi_done, wd_lo_done = sem("wd_hi_done"), sem("wd_lo_done")
        bd_hi_done, bd_lo_done = sem("bd_hi_done"), sem("bd_lo_done")
        down_done = sem("down_done")
        x1f_done = sem("x1f_done")
        y_done = sem("y_done")

        def a_raw_view(g):
            return a_raw[:, g * GB:(g + 1) * GB, :].rearrange("p b (c r) -> p c b r", r=R1)

        def a_view(t, gl):
            return t[:, gl, :, :].rearrange("p c (b r) -> p c b r", r=R1)

        def group_tokens(g):
            return slice(g * GT, (g + 1) * GT)

        block = ctx.enter_context(nc.Block())

        @block.sync
        def _(sp):
            for k in range(KT):
                sp.dma_start(x_raw[0][:, k, :], xT[0, k]).then_inc(x_landed[0][k], 16)
                sp.dma_start(w0_raw[:, k, :], w0T[k]).then_inc(w0_landed[k], 16)
                if k == 0:
                    sp.dma_start(id_sb[:], ids).then_inc(id_landed, 16)
            sp.dma_start(cst[:], consts).then_inc(cst_landed, 16)
            sp.dma_start(ar_raw[:], ar0T).then_inc(ar_landed, 16)
            for k in range(KT):
                sp.dma_start(x_raw[1][:, k, :], xT[1, k]).then_inc(x_landed[1][k], 16)
            sp.dma_start(b0_raw[:], b0T).then_inc(b0_landed, 16)

            sp.wait_ge(batch_exp_ready, 1)
            for h in range(NH):
                for b in range(h * HB, (h + 1) * HB):
                    expert = sp.value_load(batch_exp[0:1, b:b + 1], min_val=0, max_val=E1 - 1)
                    sp.dma_start(a_raw[:, b, :], a_experts[expert]).then_inc(a_landed[h], 16)

            def load_gate_up(i, u):
                sp.dma_start(w_raw[u][:], wgu[2 * i + u]).then_inc(w_landed[u], 16)

            load_gate_up(0, 0)
            load_gate_up(0, 1)
            with sp.Fori(1, FT // 2) as i:
                for u in range(2):
                    sp.wait_ge(w_lo_done, 2 * i + u - 1)
                    load_gate_up(i, u)
            sp.wait_ge(w_lo_done, FT - 2)
            load_gate_up(FT // 2, 0)

            sp.wait_ge(w_lo_done, FT)
            for m in range(KT):
                if m:
                    sp.wait_ge(wd_lo_done, m)
                sp.dma_start(wd_raw[:], wd[m]).then_inc(wd_landed, 16)
                if m >= 2:
                    for h in range(NH):
                        sp.wait_ge(y_done, NH * (m - 2) + h + 1)
                        sp.dma_start(out[m - 2, h], y_sb[:, m - 2, h * HALF:(h + 1) * HALF]).then_inc(y_stored, 16)
            for m in range(KT - 2, KT):
                for h in range(NH):
                    sp.wait_ge(y_done, NH * m + h + 1)
                    sp.dma_start(out[m, h], y_sb[:, m, h * HALF:(h + 1) * HALF]).then_inc(y_stored, 16)
            sp.wait_ge(y_stored, 16 * KT * NH)

        @block.gpsimd
        def _(pool):
            def gather(dst, table, index, landed):
                pool.indirect_dma_start(out=dst, out_offset=None, in_=table,
                                        in_offset=bass.IndirectOffsetOnAxis(ap=index, axis=0)).then_inc(landed, 16)

            pool.wait_ge(b0_hi_done, 1)
            nc.gpsimd.tensor_tensor(b0_lo[:], b0_raw[:], b0_hi[:].bitcast(F32),
                                    ALU.subtract).then_inc(b0_lo_done, 1)

            def gather_tile(i, u):
                f = 2 * i + u
                nc.gpsimd.tensor_copy(tile_idx[u][:], row_idx[:, bass.ds(f * NG, NG)]).then_inc(tile_idx_ready, 1)
                pool.wait_ge(tile_idx_ready, f + 1)
                pool.nop(nofuse=True)
                for g in range(NG):
                    gather(g_raw[u][:, g, :], ft_rows, tile_idx[u][:, g:g + 1], g_landed[u])

            pool.wait_ge(idx_ready, 1)
            pool.wait_ge(x_landed[1][KT - 1], 16)
            gather_tile(0, 0)
            gather_tile(0, 1)
            with pool.Fori(1, FT // 2) as i:
                for u in range(2):
                    pool.wait_ge(b_lo_done, 2 * i + u - 1)
                    pool.wait_ge(ad_turned, 2 * i + u - 1)
                    gather_tile(i, u)
            pool.wait_ge(b_lo_done, FT - 2)
            pool.wait_ge(ad_turned, FT - 2)
            gather_tile(FT // 2, 0)

            pool.wait_ge(up_done, HSTEPS - 2)
            for g in range(NG):
                gather(bd_raw[:, g, :], bd_rows, row_idx[:, g:g + 1], bd_landed)
            pool.wait_ge(up_done, HSTEPS)
            pool.wait_ge(tdown_done, FT)
            for m in range(KT):
                for h in range(NH):
                    part = slice(h * HALF, (h + 1) * HALF)
                    nc.gpsimd.tensor_tensor(y_sb[:, m, part], x1_hi[:, m, part].bitcast(F32),
                                            x1_lo[:, m, part].bitcast(F32), ALU.add).then_inc(x1f_done, 1)

        @block.scalar
        def _(act):
            def copy_hi(dst, src, done):
                nc.scalar.activation(dst, src, ACT.Copy).then_inc(done, 1)

            for k in range(KT):
                act.wait_ge(x_landed[0][k], 16)
                copy_hi(x_hi[0][:, k, :], x_raw[0][:, k, :], x_hi_done)
                if k:
                    act.wait_ge(w0_landed[k], 16)
                    copy_hi(w0_hi[:, k, :], w0_raw[:, k, :], w0_hi_done)
            act.wait_ge(ar_landed, 16)
            copy_hi(ar_sp[:, :, 0, :], ar_raw[:], ar_hi_done)
            for k in range(KT):
                act.wait_ge(x_landed[1][k], 16)
                copy_hi(x_hi[1][:, k, :], x_raw[1][:, k, :], x_hi_done)
            act.wait_ge(b0_landed, 16)
            copy_hi(b0_hi[:], b0_raw[:], b0_hi_done)

            def h_copy(h):
                act.wait_ge(h_done, h + 1)
                if h:
                    act.wait_ge(h_summed, h)
                nc.scalar.activation(h_part[:], ps[:, 0:TT, HC:2 * HC], ACT.Copy).then_inc(h_copied, 1)

            def exp_margin(h):
                act.wait_ge(margin_done, h + 1)
                nc.scalar.activation(e_margin[:], margin[:], ACT.Exp).then_inc(exp_done, 1)

            def a_hi_part(h, gl):
                act.wait_ge(a_landed[h], 16 * HB)
                if h == 0:
                    act.wait_ge(w0_lo_done, KT)
                else:
                    act.wait_ge(base0_done, 1)
                copy_hi(a_view(at_hi[h], gl), a_raw_view(h * GH + gl), at_hi_done)

            def turned_gh_hi(h):
                act.wait_ge(gh_turned, h + 1)
                copy_hi(ghT_hi[:, h * HALF:(h + 1) * HALF], ps[:, BANK_GHT, :], ghT_hi_done)

            def x1_hi_part(h):
                for m in range(KT):
                    act.wait_ge(x1_added, KT * h + m + 1)
                    copy_hi(x1_hi[:, m, h * HALF:(h + 1) * HALF], ps[:, BANK_OUT + m, :], x1_hi_done)

            h_copy(0)
            exp_margin(0)
            turned_gh_hi(0)
            h_copy(1)
            x1_hi_part(0)
            exp_margin(1)
            a_hi_part(0, 0)
            a_hi_part(0, 1)
            turned_gh_hi(1)
            a_hi_part(1, 0)
            a_hi_part(1, 1)
            def split_tile(i, u, used):
                act.wait_ge(w_landed[u], 16 * (i + 1))
                if used is not None:
                    act.wait_ge(up_done, used)
                copy_hi(w_hi[u][:].rearrange("p a k f -> p (a k f)"), w_raw[u][:], w_hi_done)
                act.wait_ge(g_landed[u], 16 * NG * (i + 1))
                copy_hi(b_hi[u][:], g_raw[u][:, :, 0:2 * P], b_hi_done)

            split_tile(0, 0, None)
            x1_hi_part(1)

            for h in range(NH):
                for mat in range(2):
                    act.wait_ge(t_masked, 2 * h + mat + 1)
                    copy_hi(t_hi[:, mat, h * HALF:(h + 1) * HALF], ps[:, 2 * h + mat, :], t_hi_done)

            def glu(i, u, h, first=False):
                step = 2 * (2 * i + u) + h
                act.wait_ge(gate_done, step + 1)
                if not first:
                    act.wait_ge(glu_done, step - 1)
                nc.scalar.activation(silu[h][:], ps[:, 4 + 2 * h, :], ACT.Silu).then_inc(silu_done, 1)
                act.wait_ge(glu_done, step + 1)
                copy_hi(act_hi[:, bass.ds(step * HALF, HALF)], ps[:, 5 + 2 * h, :], act_hi_done)

            def turned_ad_hi(i, u, first=False):
                f = 2 * i + u
                act.wait_ge(ad_turned, f + 1)
                if not first:
                    act.wait_ge(tdown_done, f - 1)
                copy_hi(ad_hi[u][:], ps[:, 2, :], ad_hi_done)

            def tile_work(i, u, first=False):
                split_tile(i + u, 1 - u, None if first and u == 0 else 2 * (2 * i + u))
                glu(i, u, 0, first)
                turned_ad_hi(i, u, first)
                glu(i, u, 1, first)

            tile_work(0, 0, True)
            split_tile(1, 0, 2)
            glu(0, 1, 0)
            turned_ad_hi(0, 1, True)
            glu(0, 1, 1)
            with act.Fori(1, FT // 2) as i:
                for u in range(2):
                    tile_work(i, u)
            glu(FT // 2, 0, 0)
            turned_ad_hi(FT // 2, 0)

            def down_hi(m):
                act.wait_ge(wd_landed, 16 * (m + 1))
                if m == 0:
                    act.wait_ge(b_lo_done, FT)
                    act.wait_ge(ad_turned, FT)
                elif m == 1:
                    act.wait_ge(up_done, HSTEPS)
                else:
                    act.wait_ge(down_done, NH * (m - 1))
                copy_hi(wd_hi[m % 2][:].rearrange("p f n -> p (f n)"), wd_raw[:], wd_hi_done)

            down_hi(0)
            glu(FT // 2, 0, 1)
            act.wait_ge(bd_landed, 16 * NG)
            act.wait_ge(up_done, HSTEPS)
            copy_hi(bd_hi[:], bd_raw[:], bd_hi_done)
            for h in range(NH):
                act.wait_ge(td_masked, h + 1)
                copy_hi(td_hi[:, h * HALF:(h + 1) * HALF], ps[:, h, :], td_hi_done)
            for m in range(1, KT):
                down_hi(m)

        @block.vector
        def _(dve):
            chain = [0]

            def link(ins):
                chain[0] += 1
                ins.then_inc(small_step, 1)
                dve.wait_ge(small_step, chain[0])

            def sub_lo(dst, src, hi, done):
                nc.vector.tensor_tensor(dst, src, hi.bitcast(F32), ALU.subtract).then_inc(done, 1)

            def x_lo_part(h, k):
                dve.wait_ge(x_hi_done, KT * h + k + 1)
                sub_lo(x_lo[h][:, k, :], x_raw[h][:, k, :], x_hi[h][:, k, :], x_lo_done)

            def gating(h):
                dve.wait_ge(h_copied, h + 1)
                nc.vector.tensor_tensor(h_sum[:], ps[:, 0:TT, 0:HC], h_part[:], ALU.add).then_inc(h_summed, 1)
                dve.wait_ge(h_summed, h + 1)
                link(nc.vector.scalar_tensor_tensor(
                    out=logits[:], in0=lang_hot[:, TT * h:TT * (h + 1), :],
                    scalar=LANG_BIAS, in1=h_sum[:, :, ER0:HC], op0=ALU.mult, op1=ALU.add))
                for t in range(TT):
                    last = nc.vector.max(top8[:, t, :], logits[:, t, :])
                link(last)
                if h:
                    dve.wait_ge(exp_done, h)
                nc.vector.tensor_tensor(margin[:], top8[:, :, 1], top8[:, :, 0],
                                        ALU.subtract).then_inc(margin_done, 1)
                for t in range(TT):
                    last = nc.vector.max_index(top8_idx[:, t, :], top8[:, t, :], logits[:, t, :])
                link(last)
                link(nc.vector.tensor_copy(top_f[:], top8_idx[:, :, 0:2]))
                for j in range(2):
                    last = nc.vector.tensor_tensor(
                        hot[:, j], iota8.unsqueeze(1).to_broadcast([P, TT, E0]),
                        top_f[:, :, j:j + 1].to_broadcast([P, TT, E0]), ALU.is_equal)
                link(last)
                dve.wait_ge(exp_done, h + 1)
                link(nc.vector.tensor_scalar(wsum[:], e_margin[:], 1.0, None, ALU.add))
                link(nc.vector.reciprocal(wtop[:, 1, :], wsum[:]))
                link(nc.vector.tensor_scalar(wtop[:, 0, :], wtop[:, 1, :], SCALING, None, ALU.mult))
                link(nc.vector.tensor_tensor(wtop[:, 1, :], e_margin[:], wtop[:, 0, :], ALU.mult))
                link(nc.vector.tensor_tensor(hot[:], hot[:], wtop[:].unsqueeze(3).to_broadcast([P, 2, TT, E0]),
                                             ALU.mult))
                link(nc.vector.tensor_tensor(gate[:], hot[:, 0], hot[:, 1], ALU.add))
                for t in range(TT):
                    last = nc.vector.tensor_tensor(
                        gh[h][:, t, :].rearrange("p (e r) -> p e r", r=R0),
                        h_sum[:, t, 0:ER0].rearrange("p (e r) -> p e r", r=R0),
                        gate[:, t, :].unsqueeze(2).to_broadcast([P, E0, R0]), ALU.mult)
                last.then_inc(gh_done, 1)
                dve.wait_ge(gh_done, h + 1)

            def a_lo_part(h, gl):
                dve.wait_ge(at_hi_done, GH * h + gl + 1)
                sub_lo(a_view(at_lo[h], gl), a_raw_view(h * GH + gl), a_view(at_hi[h], gl), at_lo_done)

            def turned_gh_lo(h):
                part = slice(h * HALF, (h + 1) * HALF)
                dve.wait_ge(ghT_hi_done, h + 1)
                sub_lo(ghT_lo[:, part], ps[:, BANK_GHT, :], ghT_hi[:, part], ghT_lo_done)

            def x1_part(h):
                def add(m):
                    dve.wait_ge(out0_done, KT * h + m + 1)
                    nc.vector.tensor_tensor(ps[:, BANK_OUT + m, :], ps[:, BANK_OUT + m, :], x_raw[h][:, m, :],
                                            ALU.add).then_inc(x1_added, 1)

                def lo(m):
                    part = (slice(None), m, slice(h * HALF, (h + 1) * HALF))
                    dve.wait_ge(x1_hi_done, KT * h + m + 1)
                    sub_lo(x1_lo[part], ps[:, BANK_OUT + m, :], x1_hi[part], x1_lo_done)

                add(0)
                for m in range(1, KT):
                    add(m)
                    lo(m - 1)
                lo(KT - 1)

            def w0_lo_part(k):
                if k:
                    dve.wait_ge(w0_hi_done, k)
                else:
                    dve.wait_ge(w0_hi0_done, 1)
                sub_lo(w0_lo[:, k, :], w0_raw[:, k, :], w0_hi[:, k, :], w0_lo_done)

            dve.wait_ge(w0_landed[0], 16)
            nc.vector.tensor_copy(w0_hi[:, 0, :], w0_raw[:, 0, :]).then_inc(w0_hi0_done, 1)
            w0_lo_part(0)
            x_lo_part(0, 0)

            dve.wait_ge(id_landed, 16)
            link(nc.vector.tensor_copy(idf[:], id_sb[:]))
            e_of = idf[:, NH * TT:]
            link(nc.vector.tensor_scalar(exp_f[:, 0, :], e_of, 0.0, float(E1), ALU.is_lt, ALU.mult))
            link(nc.vector.tensor_tensor(exp_f[:, 1, :], exp_f[:, 0, :], e_of, ALU.add))
            link(nc.vector.tensor_scalar(exp_f[:, 0, :], exp_f[:, 1, :], 0.0, float(E1 - 1), ALU.max, ALU.min))
            nc.vector.tensor_copy(batch_exp[:], exp_f[:, 0, NG:]).then_inc(batch_exp_ready, 1)
            dve.wait_ge(cst_landed, 16)
            link(nc.vector.tensor_scalar(row_f[:], exp_f[:, 0, 0:NG], float(R1), cst[:, C_ROFF:C_ROFF + 1],
                                         ALU.mult, ALU.add))
            nc.vector.tensor_tensor(row_idx[:].rearrange("p (f g) -> p f g", g=NG),
                                    cst[:, C_FTOFF:C_FTOFF + FT * NG].rearrange("p (f g) -> p f g", g=NG),
                                    row_f[:].unsqueeze(1).to_broadcast([P, FT, NG]),
                                    ALU.add).then_inc(idx_ready, 1)
            link(nc.vector.tensor_tensor(lang_hot[:], iota8.unsqueeze(1).to_broadcast([P, NH * TT, E0]),
                                         idf[:, 0:NH * TT].unsqueeze(2).to_broadcast([P, NH * TT, E0]),
                                         ALU.is_equal))

            for k in range(1, KT):
                x_lo_part(0, k)
                w0_lo_part(k)
            dve.wait_ge(ar_hi_done, 1)
            sub_lo(ar_sp[:, :, 1, :], ar_raw[:], ar_sp[:, :, 0, :], ar_lo_done)
            for k in range(KT):
                x_lo_part(1, k)
            gating(0)
            turned_gh_lo(0)
            x1_part(0)
            gating(1)
            a_lo_part(0, 0)
            a_lo_part(0, 1)
            turned_gh_lo(1)
            a_lo_part(1, 0)
            a_lo_part(1, 1)
            x1_part(1)

            def split_tile(i, u):
                f = 2 * i + u
                dve.wait_ge(w_hi_done, f + 1)
                sub_lo(w_lo[u][:].rearrange("p a k f -> p (a k f)"), w_raw[u][:],
                       w_hi[u][:].rearrange("p a k f -> p (a k f)"), w_lo_done)
                dve.wait_ge(b_hi_done, f + 1)
                sub_lo(b_lo[u][:], g_raw[u][:, :, 0:2 * P], b_hi[u][:], b_lo_done)

            def mask_blocks(bank, done):
                v = ps[:, bank, :].rearrange("p (g t) -> p g t", g=GH)
                nc.vector.tensor_tensor(v, v, mask.unsqueeze(1).to_broadcast([P, GH, GT]),
                                        ALU.mult).then_inc(done, 1)

            split_tile(0, 0)
            for h in range(NH):
                for mat in range(2):
                    dve.wait_ge(t_done, 2 * h + mat + 1)
                    mask_blocks(2 * h + mat, t_masked)
                for mat in range(2):
                    part = (slice(None), mat, slice(h * HALF, (h + 1) * HALF))
                    dve.wait_ge(t_hi_done, 2 * h + mat + 1)
                    sub_lo(t_lo[part], ps[:, 2 * h + mat, :], t_hi[part], t_lo_done)

            def glu(i, u, h):
                step = 2 * (2 * i + u) + h
                part = bass.ds(step * HALF, HALF)
                dve.wait_ge(silu_done, step + 1)
                dve.wait_ge(up_done, step + 1)
                nc.vector.tensor_tensor(ps[:, 5 + 2 * h, :], ps[:, 5 + 2 * h, :], silu[h][:],
                                        ALU.mult).then_inc(glu_done, 1)
                dve.wait_ge(act_hi_done, step + 1)
                sub_lo(act_lo[:, part], ps[:, 5 + 2 * h, :], act_hi[:, part], act_lo_done)

            def turned_ad_lo(i, u):
                dve.wait_ge(ad_hi_done, 2 * i + u + 1)
                sub_lo(ad_lo[u][:], ps[:, 2, :], ad_hi[u][:], ad_lo_done)

            def tile_work(i, u):
                split_tile(i + u, 1 - u)
                glu(i, u, 0)
                turned_ad_lo(i, u)
                glu(i, u, 1)

            tile_work(0, 0)
            tile_work(0, 1)
            with dve.Fori(1, FT // 2) as i:
                for u in range(2):
                    tile_work(i, u)
            glu(FT // 2, 0, 0)
            turned_ad_lo(FT // 2, 0)

            def down_lo(m):
                dve.wait_ge(wd_hi_done, m + 1)
                sub_lo(wd_lo[m % 2][:].rearrange("p f n -> p (f n)"), wd_raw[:],
                       wd_hi[m % 2][:].rearrange("p f n -> p (f n)"), wd_lo_done)

            down_lo(0)
            glu(FT // 2, 0, 1)
            dve.wait_ge(bd_hi_done, 1)
            sub_lo(bd_lo[:], bd_raw[:], bd_hi[:], bd_lo_done)
            for h in range(NH):
                dve.wait_ge(tdown_done, FT)
                mask_blocks(h, td_masked)
            for h in range(NH):
                part = slice(h * HALF, (h + 1) * HALF)
                dve.wait_ge(td_hi_done, h + 1)
                sub_lo(td_lo[:, part], ps[:, h, :], td_hi[:, part], td_lo_done)
            down_lo(1)
            for m in range(KT):
                for h in range(NH):
                    part = slice(h * HALF, (h + 1) * HALF)
                    dve.wait_ge(down_done, NH * m + h + 1)
                    dve.wait_ge(x1f_done, NH * m + h + 1)
                    nc.vector.tensor_tensor(y_sb[:, m, part], ps[:, BANK_OUT + 2 * (m % 2) + h, :],
                                            y_sb[:, m, part], ALU.add).then_inc(y_done, 1)
                if m + 2 < KT:
                    down_lo(m + 2)

        @block.tensor
        def _(pe):
            def three_passes(o, a_hi, a_lo, m_hi, m_lo, start=False, stop=False, shared=False):
                pe.matmul(o, a_hi, m_hi, start=start, stop=False, skip_group_check=shared)
                pe.matmul(o, a_hi, m_lo, start=False, stop=False, skip_group_check=shared)
                return pe.matmul(o, a_lo, m_hi, start=False, stop=stop, skip_group_check=shared)

            def lora_a_and_router(h):
                pe.wait_ge(ar_lo_done, 1)
                pe.wait_ge(x_lo_done, KT * (h + 1))
                if h:
                    pe.wait_ge(h_summed, h)
                for t in range(TT):
                    if h and t == BANK_GHT:
                        pe.wait_ge(ghT_lo_done, h)
                    tok = slice(t * P, (t + 1) * P)
                    for k in range(KT):
                        w = ar_sp[:, k, :, :].rearrange("p s c -> p (s c)")
                        pe.matmul(ps[:, t, 0:2 * HC], x_hi[h][:, k, tok], w, start=(k == 0), stop=False)
                        last = pe.matmul(ps[:, t, 0:2 * HC], x_lo[h][:, k, tok], w, start=False, stop=(k == KT - 1))
                last.then_inc(h_done, 1)

            def turn_gh(h):
                pe.wait_ge(cst_landed, 16)
                pe.wait_ge(gh_done, h + 1)
                for t in range(TT):
                    last = pe.transpose(ps[:, BANK_GHT, t * P:(t + 1) * P], gh[h][:, t, :], ident)
                last.then_inc(gh_turned, 1)

            def base0(h, ks):
                for k in ks:
                    if h == 0:
                        pe.wait_ge(x_lo_done, k + 1)
                        pe.wait_ge(w0_lo_done, k + 1)
                    for m in range(KT):
                        if h and k == 0:
                            pe.wait_ge(x1_lo_done, m + 1)
                        last = three_passes(ps[:, BANK_OUT + m, :], w0_hi[:, k, m * P:(m + 1) * P],
                                            w0_lo[:, k, m * P:(m + 1) * P], x_hi[h][:, k, :], x_lo[h][:, k, :],
                                            start=(k == 0))
                    if k == KT - 1:
                        last.then_inc(base0_done, 1)

            def lora0(h):
                pe.wait_ge(ghT_lo_done, h + 1)
                pe.wait_ge(b0_lo_done, 1)
                part = slice(h * HALF, (h + 1) * HALF)
                for m in range(KT):
                    three_passes(ps[:, BANK_OUT + m, :], b0_hi[:, m * P:(m + 1) * P], b0_lo[:, m * P:(m + 1) * P],
                                 ghT_hi[:, part], ghT_lo[:, part], stop=True).then_inc(out0_done, 1)

            def lora_t(h, mat):
                pe.wait_ge(x1_lo_done, KT * (h + 1))
                pe.wait_ge(at_lo_done, GH * (h + 1))
                if h == 0:
                    pe.wait_ge(h_summed, NH)
                else:
                    pe.wait_ge(ghT_lo_done, NH)
                for gl in range(GH):
                    for k in range(KT):
                        a = (slice(None), gl, k * 2 + mat, slice(None))
                        tok = group_tokens(h * GH + gl)
                        last = three_passes(ps[:, 2 * h + mat, gl * GT:(gl + 1) * GT], at_hi[h][a], at_lo[h][a],
                                            x1_hi[:, k, tok], x1_lo[:, k, tok],
                                            start=(k == 0), stop=(k == KT - 1))
                last.then_inc(t_done, 1)

            base0(0, range(KT // 2))
            lora_a_and_router(0)
            base0(0, range(KT // 2, KT))
            turn_gh(0)
            lora_a_and_router(1)
            lora0(0)
            base0(1, range(KT))
            turn_gh(1)
            lora_t(0, 0)
            lora0(1)
            lora_t(0, 1)
            lora_t(1, 0)
            lora_t(1, 1)

            def gate_up(i, u, h, first=False):
                step = 2 * (2 * i + u) + h
                if h == 0:
                    pe.wait_ge(w_lo_done, 2 * i + u + 1)
                half = slice(h * HALF, (h + 1) * HALF)
                for mat, (done, freed) in enumerate(((gate_done, silu_done), (up_done, act_lo_done))):
                    if not first:
                        pe.wait_ge(freed, step - 1)
                    bank = 4 + 2 * h + mat
                    for k in range(KT):
                        three_passes(ps[:, bank, :], w_hi[u][:, mat, k, :], w_lo[u][:, mat, k, :],
                                     x1_hi[:, k, half], x1_lo[:, k, half], start=(k == 0))
                    if mat == 0:
                        pe.wait_ge(b_lo_done, 2 * i + u + 1)
                        if first:
                            pe.wait_ge(t_lo_done, 2 * h + 2)
                    for gl in range(GH):
                        g = h * GH + gl
                        b = (slice(None), g, slice(mat * P, (mat + 1) * P))
                        last = three_passes(ps[:, bank, gl * GT:(gl + 1) * GT], b_hi[u][b], b_lo[u][b],
                                            t_hi[:, mat, group_tokens(g)], t_lo[:, mat, group_tokens(g)],
                                            stop=(gl == GH - 1))
                    last.then_inc(done, 1)

            def turn_a_down(i, u, first=False):
                pe.wait_ge(g_landed[u], 16 * NG * (i + 1))
                if first:
                    pe.wait_ge(t_lo_done, 2 * NH)
                else:
                    pe.wait_ge(ad_lo_done, 2 * i + u)
                for g in range(NG):
                    last = pe.transpose(ps[:, 2, g * P:(g + 1) * P], g_raw[u][:, g, 2 * P:3 * P], ident)
                last.then_inc(ad_turned, 1)

            def lora_t_down(i, u, first=False, last_tile=False):
                f = 2 * i + u
                rows = F_LAST if last_tile else P
                pe.wait_ge(ad_lo_done, f + 1)
                pe.wait_ge(act_lo_done, 2 * f + 2)
                for g in range(NG):
                    at = bass.ds(f * TOKENS + g * GT, GT)
                    last = three_passes(ps[:, g // GH, (g % GH) * GT:(g % GH + 1) * GT],
                                        ad_hi[u][0:rows, g * P:(g + 1) * P], ad_lo[u][0:rows, g * P:(g + 1) * P],
                                        act_hi[0:rows, at], act_lo[0:rows, at],
                                        start=(first and g % GH == 0), stop=last_tile, shared=True)
                last.then_inc(tdown_done, 1)

            gate_up(0, 0, 0, True)
            turn_a_down(0, 0, True)
            gate_up(0, 0, 1, True)
            gate_up(0, 1, 0)
            turn_a_down(0, 1)
            lora_t_down(0, 0, first=True)
            gate_up(0, 1, 1)
            with pe.Fori(1, FT // 2) as i:
                for u in range(2):
                    gate_up(i, u, 0)
                    turn_a_down(i, u)
                    lora_t_down(i + u - 1, 1 - u)
                    gate_up(i, u, 1)
            gate_up(FT // 2, 0, 0)
            turn_a_down(FT // 2, 0)
            lora_t_down(FT // 2 - 1, 1)
            gate_up(FT // 2, 0, 1)

            def down_base(m, h):
                bank = BANK_OUT + 2 * (m % 2) + h
                if m < 2:
                    pe.wait_ge(silu_done, HSTEPS - 1 + m)
                    pe.wait_ge(act_lo_done, HSTEPS - 1 + m)
                else:
                    pe.wait_ge(y_done, NH * (m - 2) + h + 1)
                pe.wait_ge(wd_lo_done, m + 1)
                for f in range(FT):
                    rows = F_LAST if f == FT - 1 else P
                    if m == 0 and f == FT - 1:
                        pe.wait_ge(act_lo_done, HSTEPS - 1 + h)
                    at = slice(f * TOKENS + h * HALF, f * TOKENS + (h + 1) * HALF)
                    three_passes(ps[:, bank, :], wd_hi[m % 2][0:rows, f, :], wd_lo[m % 2][0:rows, f, :],
                                 act_hi[0:rows, at], act_lo[0:rows, at], start=(f == 0))

            def down_lora(m, h):
                bank = BANK_OUT + 2 * (m % 2) + h
                pe.wait_ge(td_lo_done, NH)
                pe.wait_ge(bd_lo_done, 1)
                for gl in range(GH):
                    g = h * GH + gl
                    b = (slice(None), g, slice(m * P, (m + 1) * P))
                    last = three_passes(ps[:, bank, gl * GT:(gl + 1) * GT], bd_hi[b], bd_lo[b],
                                        td_hi[:, group_tokens(g)], td_lo[:, group_tokens(g)], stop=(gl == GH - 1))
                last.then_inc(down_done, 1)

            down_base(0, 0)
            lora_t_down(FT // 2, 0, last_tile=True)
            down_base(0, 1)
            for h in range(NH):
                down_lora(0, h)
            for m in range(1, KT):
                for h in range(NH):
                    down_base(m, h)
                    down_lora(m, h)


def kernel(**inputs):
    import numpy as np
    import concourse.bacc as bacc
    from concourse.bass_utils import run_bass_kernel_spmd

    a = {k: np.asarray(v) for k, v in inputs.items()}
    c = np.ascontiguousarray

    def f_tiles(w):
        order = np.concatenate([np.arange((FT - 1) * P, F), np.arange(F - P, F - F_LAST)])
        return np.stack([w[..., f * P:(f + 1) * P] for f in range(FT - 1)] + [w[..., order]], axis=-2)

    xT = c(a["x"].reshape(NH, HALF, KT, P).transpose(0, 2, 3, 1))
    w0T = c(a["L0_cond_W"].T.reshape(KT, P, D))
    ar = np.concatenate([a["L0_cond_A"].reshape(ER0, D), a["L0_cond_Wr"]], axis=0)
    ar0T = c(ar.T.reshape(KT, P, HC).transpose(1, 0, 2))
    b0T = c(a["L0_cond_B"].transpose(0, 2, 1).reshape(ER0, D))

    consts = np.zeros((P, C_END), np.float32)
    block = np.arange(P)[:, None] // R1 == np.arange(GT)[None, :] // BATCH_TOKENS
    consts[:, C_MASK:C_MASK + GT] = np.where(block, 0.5, 0.0)
    consts[:, C_ID:C_ID + P] = np.eye(P)
    consts[:, C_IOTA:C_IOTA + E0] = np.arange(E0)
    consts[:, C_FTOFF:C_FTOFF + FT * NG] = np.repeat(np.arange(FT) * E1 * R1, NG)
    consts[:, C_ROFF] = np.arange(P) % R1

    lang = np.repeat(a["itok_B_0_7"], BATCH_TOKENS).reshape(NH * TT, P).T
    expert = np.repeat(a["itok_B_2_6"], R1).reshape(NG, P).T
    batches = np.broadcast_to(a["itok_B_2_6"], (P, NH * HB))
    ids = c(np.concatenate([lang, expert, batches], axis=1))

    gu = np.stack([f_tiles(a["L1_cond_W_gate"].T), f_tiles(a["L1_cond_W_up"].T)])
    wgu = c(gu.reshape(2, KT, P, FT, P).transpose(3, 2, 0, 1, 4).reshape(FT, P, 2 * KT * P))
    ga = np.stack([a["L1_cond_A_gate"][0], a["L1_cond_A_up"][0]])
    a_experts = c(ga.reshape(2, E1, R1, KT, P).transpose(1, 4, 3, 0, 2).reshape(E1, P, AW))
    parts = [f_tiles(a[n][0].transpose(0, 2, 1).reshape(E1 * R1, F)) for n in ("L1_cond_B_gate", "L1_cond_B_up")]
    parts.append(f_tiles(a["L1_cond_A_down"][0].reshape(E1 * R1, F)))
    ft_rows = c(np.stack(parts, axis=2).transpose(1, 0, 2, 3).reshape(FT * E1 * R1, GW))
    wd = c(f_tiles(a["L1_cond_W_down"]).reshape(KT, P, FT, P).transpose(0, 3, 2, 1).reshape(KT, P, FT * P))
    bd_rows = c(a["L1_cond_B_down"][0].transpose(0, 2, 1).reshape(E1 * R1, D))

    arrays = {"in_xT": xT, "in_w0T": w0T, "in_ar0T": ar0T, "in_b0T": b0T, "in_consts": consts, "in_ids": ids,
              "in_wgu": wgu, "in_a_experts": a_experts, "in_ft_rows": ft_rows, "in_wd": wd, "in_bd_rows": bd_rows}
    nc = bacc.Bacc("TRN2", target_bir_lowering=False, num_devices=1)
    aps = [nc.dram_tensor(n, v.shape, mybir.dt.from_np(v.dtype), kind="ExternalInput").ap()
           for n, v in arrays.items()]
    out = nc.dram_tensor("out_yT", (KT, NH, P, HALF), F32, kind="ExternalOutput").ap()
    mlp_with_loras(nc, *aps, out)
    r = run_bass_kernel_spmd(nc, [arrays], core_ids=[0])
    y = r.results[0]["out_yT"]
    return c(y.transpose(1, 3, 0, 2)).reshape(a["x"].shape)
```

```python
from contextlib import ExitStack
from math import prod

import concourse.bass as bass
from concourse import mybir

ALU = mybir.AluOpType
ACT = mybir.ActivationFunctionType
F32 = mybir.dt.float32
F32R = mybir.dt.float32r
BF16 = mybir.dt.bfloat16
I32 = mybir.dt.int32
U32 = mybir.dt.uint32

P = 128
TOKENS = 1024
HALF = 512
NH = TOKENS // HALF
D = 512
KT = D // P
E0, R0 = 8, 16
ER0 = E0 * R0
HC = ER0 + E0
LANG_BIAS = 5.0
SCALING = 2.0
TT = HALF // P
E1, R1 = 16, 16
F = 1376
FT = -(-F // P)
F_LAST = F - (FT - 1) * P
BATCH_TOKENS = 32
GB = P // R1
GT = GB * BATCH_TOKENS
NG = TOKENS // GT
GH = NG // NH
HB = HALF // BATCH_TOKENS
AW = KT * 2 * R1
GW = 2 * P
AD_CHUNKS = (FT // 2 + 2, FT - FT // 2 - 2)
AD_LOOP = AD_CHUNKS[0] // 2
AD_STEP = HB // (2 * (AD_LOOP - 1))
LAST_COLS = [slice(gl * GT, (gl + 1) * GT) for gl in range(GH)]
WARM_UP = 7
HSTEPS = NH * FT

C_MASK, C_ID, C_IOTA, C_FTOFF, C_ROFF = 0, GT, GT + P, GT + P + E0, GT + P + E0 + FT * NG
C_END = C_ROFF + 1


def mlp_with_loras(nc, xT, w0T, ar0T, b0T, consts, ids, wgu, a_experts, ft_rows, ad_experts0, ad_experts1, wd,
                   bd_rows, out):
    with ExitStack() as ctx:
        def sem(name):
            return ctx.enter_context(nc.semaphore(name))

        cursor = [-(-nc.sbuf_base // 32) * 32]

        def region(nbytes):
            at = cursor[0]
            cursor[0] += -(-nbytes // 32) * 32
            return at

        def place(name, shape, dt, at):
            return nc.alloc_sbuf_tensor_at(name, shape, dt, offset=at)

        KB = 1024
        r_act = region(FT * TOKENS * 8)
        r_x1 = region(KT * TOKENS * 8)
        r_wraw = region(8 * KB)
        r_graw = region(2 * NG * GW * 4)
        r_adraw = region(8 * KB)
        r_silu = region(4 * KB)
        r_wsp = region(16 * KB)
        r_bsp1 = region(8 * KB)
        r_bsp0 = region(8 * KB)
        r_asp = region(8 * KB)
        r_t = region(16 * KB)

        x_raw = [place(f"x_raw{h}", [P, KT, HALF], F32, r_act + h * 8 * KB) for h in range(NH)]
        x_hi = [place(f"x_hi{h}", [P, KT, HALF], F32R, r_act + at * KB) for h, at in enumerate((16, 24))]
        x_lo = [place(f"x_lo{h}", [P, KT, HALF], F32R, r_act + at * KB) for h, at in enumerate((56, 32))]
        w0_hi = place("w0_hi", [P, KT, D], F32R, r_act + 40 * KB)
        w0_lo = place("w0_lo", [P, KT, D], F32R, r_act + 48 * KB)
        w0_raw = place("w0_raw", [P, KT, D], F32, r_act + 64 * KB)
        ghT_hi = place("ghT_hi", [P, TOKENS], F32R, r_act + 72 * KB)
        ghT_lo = place("ghT_lo", [P, TOKENS], F32R, r_act + 76 * KB)
        AR = KT * HC * 4
        ar_raw = place("ar_raw", [P, KT, HC], F32, r_act + 80 * KB)
        ar_sp = place("ar_sp", [P, KT, 2, HC], F32R, r_act + 80 * KB + AR)
        at_shape = [P, GH, KT * 2, P]
        at_hi = [place("at_hi0", at_shape, F32R, r_act + 64 * KB), place("at_hi1", at_shape, F32R, r_act + 16 * KB)]
        at_lo = [place("at_lo0", at_shape, F32R, r_adraw), place("at_lo1", at_shape, F32R, r_act + 56 * KB)]
        a_raw = place("a_raw", [P, NH * HB, AW], F32, r_t)
        b0_raw = place("b0_raw", [P, D], F32, r_bsp1)
        b0_hi = place("b0_hi", [P, D], F32R, r_bsp1 + 2 * KB)
        b0_lo = place("b0_lo", [P, D], F32R, r_bsp1 + 4 * KB)
        zeros = place("zeros", [P, HALF], BF16, r_asp + 4 * KB)
        gh = [place(f"gh{h}", [P, TT, ER0], F32, r_asp + 2 * h * KB) for h in range(NH)]
        h_part = place("h_part", [P, TT, HC], F32, r_bsp0)
        h_sum = place("h_sum", [P, TT, HC], F32, r_bsp0 + TT * HC * 4)

        act_hi = place("act_hi", [P, FT * TOKENS], F32R, r_act)
        act_lo = place("act_lo", [P, FT * TOKENS], F32R, r_act + FT * TOKENS * 4)
        ad_raw = [place(f"ad_raw{c}", [P, NH * HB, n * R1], F32,
                        (r_act + FT * TOKENS * 4 - NH * HB * n * R1 * 4, r_adraw)[c]) for c, n in enumerate(AD_CHUNKS)]
        x1_hi = place("x1_hi", [P, KT, TOKENS], F32R, r_x1)
        x1_lo = place("x1_lo", [P, KT, TOKENS], F32R, r_x1 + 16 * KB)
        w_raw = [place(f"w_raw{s}", [P, 2 * KT * P], F32, r_wraw + 4 * KB * s) for s in range(2)]
        w_hi = [place(f"w_hi{s}", [P, 2, KT, P], F32R, r_wsp + 8 * KB * s) for s in range(2)]
        w_lo = [place(f"w_lo{s}", [P, 2, KT, P], F32R, r_wsp + 8 * KB * s + 4 * KB) for s in range(2)]
        g_raw = [place(f"g_raw{s}", [P, NG, GW], F32, r_graw + NG * GW * 4 * s) for s in range(2)]
        b_hi = [place(f"b_hi{s}", [P, NG, 2 * P], F32R, (r_bsp0, r_bsp1)[s]) for s in range(2)]
        b_lo = [place(f"b_lo{s}", [P, NG, 2 * P], F32R, (r_bsp0, r_bsp1)[s] + 4 * KB) for s in range(2)]
        ad_hi = [place(f"ad_hi{s}", [P, NG * P], F32R, r_asp + 4 * KB * s) for s in range(2)]
        ad_lo = [place(f"ad_lo{s}", [P, NG * P], F32R, r_asp + 4 * KB * s + 2 * KB) for s in range(2)]
        t_hi = place("t_hi", [P, 2, TOKENS], F32R, r_t)
        t_lo = place("t_lo", [P, 2, TOKENS], F32R, r_t + 8 * KB)
        silu = [place(f"silu{h}", [P, HALF], F32, r_silu + 2 * KB * h) for h in range(NH)]

        WD = FT * P * 4
        assert r_graw + 2 * WD <= r_adraw + 4 * KB
        wd_raw = place("wd_raw", [P, FT * P], F32, r_wraw)
        wd_hi = [place(f"wd_hi{s}", [P, FT, P], F32R, (r_graw, r_wsp)[s]) for s in range(2)]
        wd_lo = [place(f"wd_lo{s}", [P, FT, P], F32R, (r_graw, r_wsp)[s] + WD) for s in range(2)]
        bd_raw = place("bd_raw", [P, NG, D], F32, r_bsp1)
        bd_hi = place("bd_hi", [P, NG, D], F32R, r_t)
        bd_lo = place("bd_lo", [P, NG, D], F32R, r_t + 8 * KB)
        td_hi = place("td_hi", [P, TOKENS], F32R, r_adraw + 4 * KB)
        td_lo = place("td_lo", [P, TOKENS], F32R, r_silu)
        y_sb = place("y_sb", [P, KT, TOKENS], F32, r_bsp0)

        def small(name, shape, dt):
            return place(name, shape, dt, region(4 * prod(shape[1:])))

        cst = small("cst", [P, C_END], F32)
        NE = NG + NH * HB
        id_sb = small("id_sb", [P, NH * TT + NE], I32)
        idf = small("idf", [P, NH * TT + NE], F32)
        exp_f = small("exp_f", [P, 2, NE], F32)
        row_f = small("row_f", [P, NG], F32)
        batch_exp = small("batch_exp", [P, NH * HB], I32)
        row_idx = small("row_idx", [P, FT * NG], I32)
        tile_idx = [small(f"tile_idx{s}", [P, NG], I32) for s in range(2)]
        lang_hot = small("lang_hot", [P, NH * TT, E0], F32)
        scratch_at = [r_bsp0 + 2 * TT * HC * 4]

        def scratch(name, shape, dt):
            at = scratch_at[0]
            scratch_at[0] += -(-4 * prod(shape[1:]) // 32) * 32
            return place(name, shape, dt, at)

        logits = scratch("logits", [P, TT, E0], F32)
        top8 = scratch("top8", [P, TT, 8], F32)
        top8_idx = scratch("top8_idx", [P, TT, 8], U32)
        top_f = scratch("top_f", [P, TT, 2], F32)
        margin = scratch("margin", [P, TT], F32)
        e_margin = scratch("e_margin", [P, TT], F32)
        wsum = scratch("wsum", [P, TT], F32)
        wtop = scratch("wtop", [P, 2, TT], F32)
        hot = scratch("hot", [P, 2, TT, E0], F32)
        gate = scratch("gate", [P, TT, E0], F32)
        assert scratch_at[0] <= r_bsp0 + 8 * KB
        assert cursor[0] <= nc.sbuf_usable_end, cursor[0]

        ps = ctx.enter_context(nc.psum_tensor("ps", [P, 8, HALF], F32))
        BANK_GHT = 3
        BANK_OUT = ((4, 5, 6, 7), (0, 1, 2, 4))
        BANK_T = ((5, 6), (7, 3))
        BANK_GU = ((0, 1), (2, 4))
        BANK_TD = (5, 6)
        BANK_Y = ((0, 2), (1, 4))
        BANK_Y_LAST = 3

        mask = cst[:, C_MASK:C_MASK + GT]
        ident = cst[:, C_ID:C_ID + P]
        iota8 = cst[:, C_IOTA:C_IOTA + E0]

        cst_landed = sem("cst_landed")
        id_landed = sem("id_landed")
        ar_landed = sem("ar_landed")
        x_landed = [[sem(f"x_landed{h}{k}") for k in range(KT)] for h in range(NH)]
        w0_landed = [sem(f"w0_landed{k}") for k in range(KT)]
        b0_landed = sem("b0_landed")
        a_landed = [sem(f"a_landed{g}") for g in range(NG)]
        w_landed = [sem(f"w_landed{s}") for s in range(2)]
        g_landed = [sem(f"g_landed{s}") for s in range(2)]
        ad_landed_sp = [sem(f"ad_landed_sp{c}") for c in range(2)]
        ad_landed_pool = [sem(f"ad_landed_pool{c}") for c in range(2)]
        wd_landed = sem("wd_landed")
        bd_landed = sem("bd_landed")
        y_stored = sem("y_stored")

        idx_ready = sem("idx_ready")
        batch_exp_ready = sem("batch_exp_ready")
        tile_idx_ready = sem("tile_idx_ready")
        small_step = sem("small_step")
        ar_hi_done, ar_lo_done = sem("ar_hi_done"), sem("ar_lo_done")
        x_hi_done, x_lo_done = sem("x_hi_done"), sem("x_lo_done")
        zeros_ready = sem("zeros_ready")
        w0_hi0_done = sem("w0_hi0_done")
        w0_hi_done, w0_lo_done = sem("w0_hi_done"), sem("w0_lo_done")
        b0_hi_done, b0_lo_done = sem("b0_hi_done"), sem("b0_lo_done")
        h_done, h_copied, h_summed = sem("h_done"), sem("h_copied"), sem("h_summed")
        margin_done = sem("margin_done")
        exp_done = sem("exp_done")
        gh_done = sem("gh_done")
        gh_turned, ghT_hi_done, ghT_lo_done = sem("gh_turned"), sem("ghT_hi_done"), sem("ghT_lo_done")
        at_hi_done = sem("at_hi_done")
        at_lo_done = [sem(f"at_lo_done{h}") for h in range(NH)]
        base0_done = sem("base0_done")
        out0_done = sem("out0_done")
        x1_added, x1_hi_done, x1_lo_done = sem("x1_added"), sem("x1_hi_done"), sem("x1_lo_done")
        t_done, t_masked, t_hi_done, t_lo_done = sem("t_done"), sem("t_masked"), sem("t_hi_done"), sem("t_lo_done")
        w_hi_done, w_lo_done = sem("w_hi_done"), sem("w_lo_done")
        b_hi_done, b_lo_done = sem("b_hi_done"), sem("b_lo_done")
        ad_hi_done, ad_lo_done = sem("ad_hi_done"), sem("ad_lo_done")
        gate_done, up_done = sem("gate_done"), sem("up_done")
        silu_done, glu_done = sem("silu_done"), sem("glu_done")
        act_hi_done, act_lo_done = sem("act_hi_done"), sem("act_lo_done")
        tdown_done, td_masked = sem("tdown_done"), sem("td_masked")
        td_hi_done, td_lo_done = sem("td_hi_done"), sem("td_lo_done")
        wd_hi_done, wd_lo_done = sem("wd_hi_done"), sem("wd_lo_done")
        bd_hi_done, bd_lo_done = sem("bd_hi_done"), sem("bd_lo_done")
        down_done = sem("down_done")
        x1f_done = sem("x1f_done")
        y_done = sem("y_done")

        def down_bank(m, h, cols):
            return BANK_Y[m % 2][h] if (m, h) != (KT - 1, NH - 1) or cols.start == 0 else BANK_Y_LAST

        def a_raw_view(g):
            return a_raw[:, g * GB:(g + 1) * GB, :].rearrange("p b (c r) -> p c b r", r=R1)

        def a_view(t, gl):
            return t[:, gl, :, :].rearrange("p c (b r) -> p c b r", r=R1)

        def group_tokens(g):
            return slice(g * GT, (g + 1) * GT)

        def load_a(eng, g):
            for b in range(g * GB, (g + 1) * GB):
                expert = eng.value_load(batch_exp[0:1, b:b + 1], min_val=0, max_val=E1 - 1)
                eng.dma_start(a_raw[:, b, :], a_experts[expert]).then_inc(a_landed[g], 16)

        def load_a_down(eng, chunk, b, landed):
            expert = eng.value_load(batch_exp[0:1, bass.ds(b, 1)], min_val=0, max_val=E1 - 1)
            eng.dma_start(ad_raw[chunk][:, bass.ds(b, 1), :],
                          (ad_experts0, ad_experts1)[chunk][expert]).then_inc(landed, 16)

        def ad_raw_view(f, chunk):
            return ad_raw[chunk][:, :, bass.ds(f * R1 - chunk * AD_CHUNKS[0] * R1, R1)]

        def ad_view(t):
            return t[:].rearrange("p (b r) -> p b r", r=R1)

        block = ctx.enter_context(nc.Block())

        @block.sync
        def _(sp):
            def load_x(h, k):
                sp.dma_start(x_raw[h][:, k, :], xT[h, k]).then_inc(x_landed[h][k], 16)

            def load_w0(k):
                sp.dma_start(w0_raw[:, k, :], w0T[k]).then_inc(w0_landed[k], 16)

            load_x(0, 0)
            load_w0(0)
            sp.dma_start(id_sb[:], ids).then_inc(id_landed, 16)
            load_x(0, 1)
            load_w0(1)
            for k in range(KT // 2, KT):
                load_x(0, k)
            sp.dma_start(ar_raw[:], ar0T).then_inc(ar_landed, 16)
            for k in range(KT // 2, KT):
                load_w0(k)
            sp.dma_start(cst[:], consts).then_inc(cst_landed, 16)
            for k in range(KT):
                load_x(1, k)
            sp.dma_start(b0_raw[:], b0T).then_inc(b0_landed, 16)

            sp.wait_ge(batch_exp_ready, 1)
            for g in range(NG - 1):
                load_a(sp, g)

            def load_gate_up(i, u):
                sp.dma_start(w_raw[u][:], wgu[2 * i + u]).then_inc(w_landed[u], 16)

            load_gate_up(0, 0)
            load_gate_up(0, 1)
            sp.wait_ge(base0_done, NH)
            with sp.Fori(0, HB // 2) as b:
                load_a_down(sp, 0, b, ad_landed_sp[0])
            sp.wait_ge(w_lo_done, 1)
            load_gate_up(1, 0)
            with sp.Fori(HB // 2, HB) as b:
                load_a_down(sp, 0, b, ad_landed_sp[0])
            sp.wait_ge(t_done, 2)
            with sp.Fori(1, AD_LOOP) as i:
                for u in range(2):
                    for n in range(AD_STEP):
                        load_a_down(sp, 1, ((i - 1) * 2 + u) * AD_STEP + n, ad_landed_sp[1])
                    sp.wait_ge(w_lo_done, 2 * i + u)
                    load_gate_up(i + u, 1 - u)
            with sp.Fori(AD_LOOP, FT // 2) as i:
                for u in range(2):
                    sp.wait_ge(w_lo_done, 2 * i + u)
                    load_gate_up(i + u, 1 - u)

            def store(m, h, parts=(slice(0, HALF),)):
                for n, cols in enumerate(parts):
                    sp.wait_ge(y_done, NH * m + h + n + 1)
                    sp.dma_start(out[m, h][:, cols], y_sb[:, m, h * HALF + cols.start:h * HALF + cols.stop]
                                 ).then_inc(y_stored, 16)

            sp.wait_ge(w_lo_done, FT)
            for m in range(KT):
                if m:
                    sp.wait_ge(wd_lo_done, m)
                sp.dma_start(wd_raw[:], wd[m]).then_inc(wd_landed, 16)
                if m >= 2:
                    store(m - 2, 0)
                    store(m - 2, 1)
            store(KT - 2, 0)
            store(KT - 2, 1)
            store(KT - 1, 0)
            store(KT - 1, 1, LAST_COLS)
            sp.wait_ge(y_stored, 16 * (KT * NH - 1 + len(LAST_COLS)))

        @block.gpsimd
        def _(pool):
            def gather(dst, table, index, landed):
                pool.indirect_dma_start(out=dst, out_offset=None, in_=table,
                                        in_offset=bass.IndirectOffsetOnAxis(ap=index, axis=0)).then_inc(landed, 16)

            def gather_tile(i, u):
                f = 2 * i + u
                nc.gpsimd.tensor_copy(tile_idx[u][:], row_idx[:, bass.ds(f * NG, NG)]).then_inc(tile_idx_ready, 1)
                pool.wait_ge(tile_idx_ready, f + 1)
                pool.nop(nofuse=True)
                for g in range(NG):
                    gather(g_raw[u][:, g, :], ft_rows, tile_idx[u][:, g:g + 1], g_landed[u])

            pool.wait_ge(batch_exp_ready, 1)
            pool.wait_ge(x_landed[1][KT - 1], 16)
            load_a(pool, NG - 1)
            pool.wait_ge(b0_hi_done, 1)
            nc.gpsimd.tensor_tensor(b0_lo[:], b0_raw[:], b0_hi[:].bitcast(F32),
                                    ALU.subtract).then_inc(b0_lo_done, 1)
            pool.wait_ge(idx_ready, 1)
            gather_tile(0, 0)
            gather_tile(0, 1)
            for gl in range(GH):
                pool.wait_ge(at_hi_done, GH + gl + 1)
                nc.gpsimd.tensor_tensor(a_view(at_lo[1], gl), a_raw_view(GH + gl), a_view(at_hi[1], gl).bitcast(F32),
                                        ALU.subtract).then_inc(at_lo_done[1], 1)
            pool.wait_ge(base0_done, NH)
            with pool.Fori(HB, HB + HB // 2) as b:
                load_a_down(pool, 0, b, ad_landed_pool[0])
            pool.wait_ge(b_lo_done, 1)
            gather_tile(1, 0)
            with pool.Fori(HB + HB // 2, 2 * HB) as b:
                load_a_down(pool, 0, b, ad_landed_pool[0])
            pool.wait_ge(t_done, 2)
            with pool.Fori(1, AD_LOOP) as i:
                for u in range(2):
                    for n in range(AD_STEP):
                        load_a_down(pool, 1, ((i - 1) * 2 + u) * AD_STEP + n + HB, ad_landed_pool[1])
                    pool.wait_ge(b_lo_done, 2 * i + u)
                    gather_tile(i + u, 1 - u)
            with pool.Fori(AD_LOOP, FT // 2) as i:
                for u in range(2):
                    pool.wait_ge(b_lo_done, 2 * i + u)
                    gather_tile(i + u, 1 - u)

            pool.wait_ge(up_done, HSTEPS - 2)
            for g in range(NG):
                gather(bd_raw[:, g, :], bd_rows, row_idx[:, g:g + 1], bd_landed)
            pool.wait_ge(up_done, HSTEPS)
            pool.wait_ge(tdown_done, FT)
            for m in range(KT):
                for h in range(NH):
                    part = slice(h * HALF, (h + 1) * HALF)
                    nc.gpsimd.tensor_tensor(y_sb[:, m, part], x1_hi[:, m, part].bitcast(F32),
                                            x1_lo[:, m, part].bitcast(F32), ALU.add).then_inc(x1f_done, 1)

        @block.scalar
        def _(act):
            def copy_hi(dst, src, done):
                nc.scalar.activation(dst, src, ACT.Copy).then_inc(done, 1)

            def x_hi_part(h, k):
                act.wait_ge(x_landed[h][k], 16)
                copy_hi(x_hi[h][:, k, :], x_raw[h][:, k, :], x_hi_done)

            def w0_hi_part(k):
                act.wait_ge(w0_landed[k], 16)
                copy_hi(w0_hi[:, k, :], w0_raw[:, k, :], w0_hi_done)

            x_hi_part(0, 0)
            x_hi_part(0, 1)
            w0_hi_part(1)
            for k in range(KT // 2, KT):
                x_hi_part(0, k)
            act.wait_ge(ar_landed, 16)
            copy_hi(ar_sp[:, :, 0, :], ar_raw[:], ar_hi_done)
            for k in range(KT // 2, KT):
                w0_hi_part(k)
            for k in range(KT):
                x_hi_part(1, k)
            act.wait_ge(b0_landed, 16)
            copy_hi(b0_hi[:], b0_raw[:], b0_hi_done)

            def h_copy(h):
                act.wait_ge(h_done, h + 1)
                if h:
                    act.wait_ge(h_summed, h)
                nc.scalar.activation(h_part[:], ps[:, 0:TT, HC:2 * HC], ACT.Copy).then_inc(h_copied, 1)

            def exp_margin(h):
                act.wait_ge(margin_done, h + 1)
                nc.scalar.activation(e_margin[:], margin[:], ACT.Exp).then_inc(exp_done, 1)

            def a_hi_part(h, gl):
                act.wait_ge(a_landed[h * GH + gl], 16 * GB)
                if h == 0:
                    act.wait_ge(w0_lo_done, KT)
                else:
                    act.wait_ge(base0_done, 1)
                copy_hi(a_view(at_hi[h], gl), a_raw_view(h * GH + gl), at_hi_done)

            def turned_gh_hi(h):
                act.wait_ge(gh_turned, h + 1)
                copy_hi(ghT_hi[:, h * HALF:(h + 1) * HALF], ps[:, BANK_GHT, :], ghT_hi_done)

            def x1_hi_part(h):
                for m in range(KT):
                    act.wait_ge(x1_added, KT * h + m + 1)
                    copy_hi(x1_hi[:, m, h * HALF:(h + 1) * HALF], ps[:, BANK_OUT[h][m], :], x1_hi_done)

            h_copy(0)
            exp_margin(0)
            turned_gh_hi(0)
            h_copy(1)
            x1_hi_part(0)
            exp_margin(1)
            a_hi_part(0, 0)
            a_hi_part(0, 1)
            a_hi_part(1, 0)
            a_hi_part(1, 1)
            turned_gh_hi(1)
            x1_hi_part(1)

            def split_tile(i, u, used):
                act.wait_ge(w_landed[u], 16 * (i + 1))
                if used is not None:
                    act.wait_ge(up_done, used)
                copy_hi(w_hi[u][:].rearrange("p a k f -> p (a k f)"), w_raw[u][:], w_hi_done)
                act.wait_ge(g_landed[u], 16 * NG * (i + 1))
                copy_hi(b_hi[u][:], g_raw[u][:], b_hi_done)

            split_tile(0, 0, None)

            for h in range(NH):
                for mat in range(2):
                    act.wait_ge(t_masked, 2 * h + mat + 1)
                    copy_hi(t_hi[:, mat, h * HALF:(h + 1) * HALF], ps[:, BANK_T[h][mat], :], t_hi_done)

            def glu(i, u, h, first=False):
                step = 2 * (2 * i + u) + h
                act.wait_ge(gate_done, step + 1)
                if not first:
                    act.wait_ge(glu_done, step - 1)
                nc.scalar.activation(silu[h][:], ps[:, BANK_GU[h][0], :], ACT.Silu).then_inc(silu_done, 1)
                act.wait_ge(glu_done, step + 1)
                copy_hi(act_hi[:, bass.ds(step * HALF, HALF)], ps[:, BANK_GU[h][1], :], act_hi_done)

            def a_down_hi(i, u, chunk, first=False):
                if not first:
                    act.wait_ge(tdown_done, 2 * i + u - 1)
                copy_hi(ad_view(ad_hi[u]), ad_raw_view(2 * i + u, chunk), ad_hi_done)

            def a_down_landed(chunk):
                act.wait_ge(ad_landed_sp[chunk], 16 * HB)
                act.wait_ge(ad_landed_pool[chunk], 16 * HB)

            def tile_work(i, u, chunk):
                split_tile(i + u, 1 - u, 2 * (2 * i + u))
                glu(i, u, 0)
                a_down_hi(i + u, 1 - u, chunk)
                glu(i, u, 1)

            split_tile(0, 1, None)
            glu(0, 0, 0, True)
            glu(0, 0, 1, True)
            split_tile(1, 0, 2)
            a_down_landed(0)
            a_down_hi(0, 0, 0, True)
            a_down_hi(0, 1, 0, True)
            glu(0, 1, 0)
            a_down_hi(1, 0, 0)
            glu(0, 1, 1)
            with act.Fori(1, AD_LOOP) as i:
                for u in range(2):
                    tile_work(i, u, 0)
            a_down_landed(1)
            with act.Fori(AD_LOOP, FT // 2) as i:
                for u in range(2):
                    tile_work(i, u, 1)
            glu(FT // 2, 0, 0)

            def down_hi(m):
                act.wait_ge(wd_landed, 16 * (m + 1))
                if m == 0:
                    act.wait_ge(b_lo_done, FT)
                    act.wait_ge(ad_lo_done, FT)
                elif m == 1:
                    act.wait_ge(up_done, HSTEPS)
                else:
                    act.wait_ge(down_done, NH * (m - 1))
                copy_hi(wd_hi[m % 2][:].rearrange("p f n -> p (f n)"), wd_raw[:], wd_hi_done)

            down_hi(0)
            glu(FT // 2, 0, 1)
            act.wait_ge(bd_landed, 16 * NG)
            act.wait_ge(up_done, HSTEPS)
            copy_hi(bd_hi[:], bd_raw[:], bd_hi_done)
            for h in range(NH):
                act.wait_ge(td_masked, h + 1)
                copy_hi(td_hi[:, h * HALF:(h + 1) * HALF], ps[:, BANK_TD[h], :], td_hi_done)
            for m in range(1, KT):
                down_hi(m)

        @block.vector
        def _(dve):
            chain = [0]

            def link(ins):
                chain[0] += 1
                ins.then_inc(small_step, 1)
                dve.wait_ge(small_step, chain[0])

            def sub_lo(dst, src, hi, done):
                nc.vector.tensor_tensor(dst, src, hi.bitcast(F32), ALU.subtract).then_inc(done, 1)

            def x_lo_part(h, k):
                dve.wait_ge(x_hi_done, KT * h + k + 1)
                sub_lo(x_lo[h][:, k, :], x_raw[h][:, k, :], x_hi[h][:, k, :], x_lo_done)

            def sum_h(h):
                dve.wait_ge(h_copied, h + 1)
                nc.vector.tensor_tensor(h_sum[:], ps[:, 0:TT, 0:HC], h_part[:], ALU.add).then_inc(h_summed, 1)
                dve.wait_ge(h_summed, h + 1)

            def gating(h):
                link(nc.vector.scalar_tensor_tensor(
                    out=logits[:], in0=lang_hot[:, TT * h:TT * (h + 1), :],
                    scalar=LANG_BIAS, in1=h_sum[:, :, ER0:HC], op0=ALU.mult, op1=ALU.add))
                for t in range(TT):
                    last = nc.vector.max(top8[:, t, :], logits[:, t, :])
                link(last)
                if h:
                    dve.wait_ge(exp_done, h)
                nc.vector.tensor_tensor(margin[:], top8[:, :, 1], top8[:, :, 0],
                                        ALU.subtract).then_inc(margin_done, 1)
                for t in range(TT):
                    last = nc.vector.max_index(top8_idx[:, t, :], top8[:, t, :], logits[:, t, :])
                link(last)
                link(nc.vector.tensor_copy(top_f[:], top8_idx[:, :, 0:2]))
                for j in range(2):
                    last = nc.vector.tensor_tensor(
                        hot[:, j], iota8.unsqueeze(1).to_broadcast([P, TT, E0]),
                        top_f[:, :, j:j + 1].to_broadcast([P, TT, E0]), ALU.is_equal)
                link(last)
                dve.wait_ge(exp_done, h + 1)
                link(nc.vector.tensor_scalar(wsum[:], e_margin[:], 1.0, None, ALU.add))
                link(nc.vector.reciprocal(wtop[:, 1, :], wsum[:]))
                link(nc.vector.tensor_scalar(wtop[:, 0, :], wtop[:, 1, :], SCALING, None, ALU.mult))
                link(nc.vector.tensor_tensor(wtop[:, 1, :], e_margin[:], wtop[:, 0, :], ALU.mult))
                link(nc.vector.tensor_tensor(hot[:], hot[:], wtop[:].unsqueeze(3).to_broadcast([P, 2, TT, E0]),
                                             ALU.mult))
                link(nc.vector.tensor_tensor(gate[:], hot[:, 0], hot[:, 1], ALU.add))
                for t in range(TT):
                    nc.vector.tensor_tensor(
                        gh[h][:, t, :].rearrange("p (e r) -> p e r", r=R0),
                        h_sum[:, t, 0:ER0].rearrange("p (e r) -> p e r", r=R0),
                        gate[:, t, :].unsqueeze(2).to_broadcast([P, E0, R0]), ALU.mult).then_inc(gh_done, 1)
                dve.wait_ge(gh_done, TT * (h + 1))

            def a_lo_part(h):
                for gl in range(GH):
                    dve.wait_ge(at_hi_done, GH * h + gl + 1)
                    sub_lo(a_view(at_lo[h], gl), a_raw_view(h * GH + gl), a_view(at_hi[h], gl), at_lo_done[h])

            def turned_gh_lo(h):
                part = slice(h * HALF, (h + 1) * HALF)
                dve.wait_ge(ghT_hi_done, h + 1)
                sub_lo(ghT_lo[:, part], ps[:, BANK_GHT, :], ghT_hi[:, part], ghT_lo_done)

            def x1_part(h):
                def add(m):
                    dve.wait_ge(out0_done, KT * h + m + 1)
                    bank = BANK_OUT[h][m]
                    nc.vector.tensor_tensor(ps[:, bank, :], ps[:, bank, :], x_raw[h][:, m, :],
                                            ALU.add).then_inc(x1_added, 1)

                def lo(m):
                    part = (slice(None), m, slice(h * HALF, (h + 1) * HALF))
                    dve.wait_ge(x1_hi_done, KT * h + m + 1)
                    sub_lo(x1_lo[part], ps[:, BANK_OUT[h][m], :], x1_hi[part], x1_lo_done)

                add(0)
                for m in range(1, KT):
                    add(m)
                    lo(m - 1)
                lo(KT - 1)

            def w0_lo_part(k):
                if k:
                    dve.wait_ge(w0_hi_done, k)
                else:
                    dve.wait_ge(w0_hi0_done, 2)
                sub_lo(w0_lo[:, k, :], w0_raw[:, k, :], w0_hi[:, k, :], w0_lo_done)

            nc.vector.memset(zeros[:], 0.0).then_inc(zeros_ready, 1)
            dve.wait_ge(w0_landed[0], 16)
            for part in (slice(0, D // 2), slice(D // 2, D)):
                nc.vector.tensor_copy(w0_hi[:, 0, part], w0_raw[:, 0, part]).then_inc(w0_hi0_done, 1)
            w0_lo_part(0)
            x_lo_part(0, 0)

            dve.wait_ge(id_landed, 16)
            link(nc.vector.tensor_copy(idf[:], id_sb[:]))
            e_of = idf[:, NH * TT:]
            link(nc.vector.tensor_scalar(exp_f[:, 0, :], e_of, 0.0, float(E1), ALU.is_lt, ALU.mult))
            link(nc.vector.tensor_tensor(exp_f[:, 1, :], exp_f[:, 0, :], e_of, ALU.add))
            link(nc.vector.tensor_scalar(exp_f[:, 0, :], exp_f[:, 1, :], 0.0, float(E1 - 1), ALU.max, ALU.min))
            nc.vector.tensor_copy(batch_exp[:], exp_f[:, 0, NG:]).then_inc(batch_exp_ready, 1)
            x_lo_part(0, 1)
            w0_lo_part(1)
            for k in range(KT // 2, KT):
                x_lo_part(0, k)
            dve.wait_ge(ar_hi_done, 1)
            sub_lo(ar_sp[:, :, 1, :], ar_raw[:], ar_sp[:, :, 0, :], ar_lo_done)
            for k in range(KT // 2, KT):
                w0_lo_part(k)
            dve.wait_ge(cst_landed, 16)
            link(nc.vector.tensor_scalar(row_f[:], exp_f[:, 0, 0:NG], float(R1), cst[:, C_ROFF:C_ROFF + 1],
                                         ALU.mult, ALU.add))
            nc.vector.tensor_tensor(row_idx[:].rearrange("p (f g) -> p f g", g=NG),
                                    cst[:, C_FTOFF:C_FTOFF + FT * NG].rearrange("p (f g) -> p f g", g=NG),
                                    row_f[:].unsqueeze(1).to_broadcast([P, FT, NG]),
                                    ALU.add).then_inc(idx_ready, 1)
            link(nc.vector.tensor_tensor(lang_hot[:], iota8.unsqueeze(1).to_broadcast([P, NH * TT, E0]),
                                         idf[:, 0:NH * TT].unsqueeze(2).to_broadcast([P, NH * TT, E0]),
                                         ALU.is_equal))

            for k in range(KT):
                x_lo_part(1, k)
            sum_h(0)
            gating(0)
            turned_gh_lo(0)
            sum_h(1)
            x1_part(0)
            gating(1)
            a_lo_part(0)
            turned_gh_lo(1)
            x1_part(1)

            def split_tile(i, u):
                f = 2 * i + u
                dve.wait_ge(w_hi_done, f + 1)
                sub_lo(w_lo[u][:].rearrange("p a k f -> p (a k f)"), w_raw[u][:],
                       w_hi[u][:].rearrange("p a k f -> p (a k f)"), w_lo_done)
                dve.wait_ge(b_hi_done, f + 1)
                sub_lo(b_lo[u][:], g_raw[u][:], b_hi[u][:], b_lo_done)

            def mask_blocks(bank, done):
                v = ps[:, bank, :].rearrange("p (g t) -> p g t", g=GH)
                nc.vector.tensor_tensor(v, v, mask.unsqueeze(1).to_broadcast([P, GH, GT]),
                                        ALU.mult).then_inc(done, 1)

            split_tile(0, 0)
            dve.wait_ge(at_lo_done[1], GH)
            for h in range(NH):
                for mat in range(2):
                    dve.wait_ge(t_done, 2 * h + mat + 1)
                    mask_blocks(BANK_T[h][mat], t_masked)
                for mat in range(2):
                    part = (slice(None), mat, slice(h * HALF, (h + 1) * HALF))
                    dve.wait_ge(t_hi_done, 2 * h + mat + 1)
                    sub_lo(t_lo[part], ps[:, BANK_T[h][mat], :], t_hi[part], t_lo_done)

            def glu(i, u, h):
                step = 2 * (2 * i + u) + h
                part = bass.ds(step * HALF, HALF)
                dve.wait_ge(silu_done, step + 1)
                dve.wait_ge(up_done, step + 1)
                nc.vector.tensor_tensor(ps[:, BANK_GU[h][1], :], ps[:, BANK_GU[h][1], :], silu[h][:],
                                        ALU.mult).then_inc(glu_done, 1)
                dve.wait_ge(act_hi_done, step + 1)
                sub_lo(act_lo[:, part], ps[:, BANK_GU[h][1], :], act_hi[:, part], act_lo_done)

            def a_down_lo(i, u, chunk):
                dve.wait_ge(ad_hi_done, 2 * i + u + 1)
                sub_lo(ad_view(ad_lo[u]), ad_raw_view(2 * i + u, chunk), ad_view(ad_hi[u]), ad_lo_done)

            def tile_work(i, u, chunk):
                split_tile(i + u, 1 - u)
                glu(i, u, 0)
                a_down_lo(i + u, 1 - u, chunk)
                glu(i, u, 1)

            split_tile(0, 1)
            glu(0, 0, 0)
            glu(0, 0, 1)
            split_tile(1, 0)
            a_down_lo(0, 0, 0)
            a_down_lo(0, 1, 0)
            glu(0, 1, 0)
            a_down_lo(1, 0, 0)
            glu(0, 1, 1)
            with dve.Fori(1, AD_LOOP) as i:
                for u in range(2):
                    tile_work(i, u, 0)
            with dve.Fori(AD_LOOP, FT // 2) as i:
                for u in range(2):
                    tile_work(i, u, 1)
            glu(FT // 2, 0, 0)

            def down_lo(m):
                dve.wait_ge(wd_hi_done, m + 1)
                sub_lo(wd_lo[m % 2][:].rearrange("p f n -> p (f n)"), wd_raw[:],
                       wd_hi[m % 2][:].rearrange("p f n -> p (f n)"), wd_lo_done)

            down_lo(0)
            glu(FT // 2, 0, 1)
            dve.wait_ge(bd_hi_done, 1)
            sub_lo(bd_lo[:], bd_raw[:], bd_hi[:], bd_lo_done)
            for h in range(NH):
                dve.wait_ge(tdown_done, FT)
                mask_blocks(BANK_TD[h], td_masked)
            for h in range(NH):
                part = slice(h * HALF, (h + 1) * HALF)
                dve.wait_ge(td_hi_done, h + 1)
                sub_lo(td_lo[:, part], ps[:, BANK_TD[h], :], td_hi[:, part], td_lo_done)
            down_lo(1)
            for m in range(KT):
                for h in range(NH):
                    last = (m, h) == (KT - 1, NH - 1)
                    dve.wait_ge(x1f_done, NH * m + h + 1)
                    for n, cols in enumerate(LAST_COLS if last else [slice(0, HALF)]):
                        part = slice(h * HALF + cols.start, h * HALF + cols.stop)
                        dve.wait_ge(down_done, NH * m + h + n + 1)
                        nc.vector.tensor_tensor(y_sb[:, m, part], ps[:, down_bank(m, h, cols), cols],
                                                y_sb[:, m, part], ALU.add).then_inc(y_done, 1)
                if m + 2 < KT:
                    down_lo(m + 2)

        @block.tensor
        def _(pe):
            def three_passes(o, a_hi, a_lo, m_hi, m_lo, start=False, stop=False, shared=False):
                pe.matmul(o, a_hi, m_hi, start=start, stop=False, skip_group_check=shared)
                pe.matmul(o, a_hi, m_lo, start=False, stop=False, skip_group_check=shared)
                return pe.matmul(o, a_lo, m_hi, start=False, stop=stop, skip_group_check=shared)

            def lora_a_and_router(h):
                pe.wait_ge(ar_lo_done, 1)
                pe.wait_ge(x_lo_done, KT * (h + 1))
                if h:
                    pe.wait_ge(h_summed, h)
                for t in range(TT):
                    if h and t == BANK_GHT:
                        pe.wait_ge(ghT_lo_done, h)
                    tok = slice(t * P, (t + 1) * P)
                    for k in range(KT):
                        w = ar_sp[:, k, :, :].rearrange("p s c -> p (s c)")
                        pe.matmul(ps[:, t, 0:2 * HC], x_hi[h][:, k, tok], w, start=(k == 0), stop=False)
                        last = pe.matmul(ps[:, t, 0:HC], x_lo[h][:, k, tok], w[:, 0:HC], start=False,
                                         stop=(k == KT - 1))
                last.then_inc(h_done, 1)

            def turn_gh(h):
                pe.wait_ge(cst_landed, 16)
                for t in range(TT):
                    pe.wait_ge(gh_done, TT * h + t + 1)
                    last = pe.transpose(ps[:, BANK_GHT, t * P:(t + 1) * P], gh[h][:, t, :], ident)
                last.then_inc(gh_turned, 1)

            def base0(h, ks):
                for k in ks:
                    if h == 0 and k == 0:
                        pe.wait_ge(x_hi_done, 1)
                        for w, x, operand_done in ((w0_hi, x_hi[0], w0_hi0_done), (w0_lo, x_hi[0], w0_lo_done),
                                                   (w0_hi, x_lo[0], x_lo_done)):
                            pe.wait_ge(operand_done, 1)
                            for m in range(KT):
                                if operand_done is w0_hi0_done and m == KT // 2:
                                    pe.wait_ge(w0_hi0_done, 2)
                                pe.matmul(ps[:, BANK_OUT[0][m], :], w[:, 0, m * P:(m + 1) * P], x[:, 0, :],
                                          start=(operand_done is w0_hi0_done), stop=False)
                        continue
                    if h == 0:
                        pe.wait_ge(x_lo_done, k + 1)
                        pe.wait_ge(w0_lo_done, k + 1)
                    for m in range(KT):
                        if h and k == 0 and m == 0:
                            pe.wait_ge(h_summed, NH)
                        if h and k == 0 and BANK_OUT[1][m] in BANK_OUT[0]:
                            pe.wait_ge(x1_lo_done, BANK_OUT[0].index(BANK_OUT[1][m]) + 1)
                        last = three_passes(ps[:, BANK_OUT[h][m], :], w0_hi[:, k, m * P:(m + 1) * P],
                                            w0_lo[:, k, m * P:(m + 1) * P], x_hi[h][:, k, :], x_lo[h][:, k, :],
                                            start=(k == 0))
                    if k == KT - 1:
                        last.then_inc(base0_done, 1)

            def lora0(h):
                pe.wait_ge(ghT_lo_done, h + 1)
                pe.wait_ge(b0_lo_done, 1)
                part = slice(h * HALF, (h + 1) * HALF)
                for m in range(KT):
                    three_passes(ps[:, BANK_OUT[h][m], :], b0_hi[:, m * P:(m + 1) * P], b0_lo[:, m * P:(m + 1) * P],
                                 ghT_hi[:, part], ghT_lo[:, part], stop=True).then_inc(out0_done, 1)

            def lora_t(h, mat):
                pe.wait_ge(at_lo_done[h], GH)
                if h:
                    pe.wait_ge(ghT_lo_done, NH)
                for gl in range(GH):
                    for k in range(KT):
                        pe.wait_ge(x1_lo_done, KT * h + k + 1)
                        a = (slice(None), gl, k * 2 + mat, slice(None))
                        tok = group_tokens(h * GH + gl)
                        last = three_passes(ps[:, BANK_T[h][mat], gl * GT:(gl + 1) * GT], at_hi[h][a], at_lo[h][a],
                                            x1_hi[:, k, tok], x1_lo[:, k, tok],
                                            start=(k == 0), stop=(k == KT - 1))
                last.then_inc(t_done, 1)

            pe.wait_ge(zeros_ready, 1)
            for _ in range(WARM_UP):
                pe.matmul(ps[:, 0, :], zeros[:, 0:P], zeros[:], start=True, stop=True)

            base0(0, range(KT // 2))
            lora_a_and_router(0)
            base0(0, range(KT // 2, KT))
            turn_gh(0)
            lora_a_and_router(1)
            lora0(0)
            base0(1, range(KT))
            turn_gh(1)
            lora_t(0, 0)
            lora0(1)
            lora_t(0, 1)
            lora_t(1, 0)
            lora_t(1, 1)

            def gate_up(i, u, h, first=False):
                step = 2 * (2 * i + u) + h
                if h == 0:
                    pe.wait_ge(w_lo_done, 2 * i + u + 1)
                half = slice(h * HALF, (h + 1) * HALF)
                for mat, (done, freed) in enumerate(((gate_done, silu_done), (up_done, act_lo_done))):
                    if not first:
                        pe.wait_ge(freed, step - 1)
                    bank = BANK_GU[h][mat]
                    for k in range(KT):
                        three_passes(ps[:, bank, :], w_hi[u][:, mat, k, :], w_lo[u][:, mat, k, :],
                                     x1_hi[:, k, half], x1_lo[:, k, half], start=(k == 0))
                    if mat == 0:
                        pe.wait_ge(b_lo_done, 2 * i + u + 1)
                        if first:
                            pe.wait_ge(t_lo_done, 2 * h + 2)
                    for gl in range(GH):
                        g = h * GH + gl
                        b = (slice(None), g, slice(mat * P, (mat + 1) * P))
                        last = three_passes(ps[:, bank, gl * GT:(gl + 1) * GT], b_hi[u][b], b_lo[u][b],
                                            t_hi[:, mat, group_tokens(g)], t_lo[:, mat, group_tokens(g)],
                                            stop=(gl == GH - 1))
                    last.then_inc(done, 1)

            def lora_t_down(i, u, first=False, last_tile=False):
                f = 2 * i + u
                rows = F_LAST if last_tile else P
                if first:
                    pe.wait_ge(t_lo_done, 2 * NH)
                pe.wait_ge(ad_lo_done, f + 1)
                pe.wait_ge(act_lo_done, 2 * f + 2)
                for g in range(NG):
                    at = bass.ds(f * TOKENS + g * GT, GT)
                    last = three_passes(ps[:, BANK_TD[g // GH], (g % GH) * GT:(g % GH + 1) * GT],
                                        ad_hi[u][0:rows, g * P:(g + 1) * P], ad_lo[u][0:rows, g * P:(g + 1) * P],
                                        act_hi[0:rows, at], act_lo[0:rows, at],
                                        start=(first and g % GH == 0), stop=last_tile, shared=True)
                last.then_inc(tdown_done, 1)

            gate_up(0, 0, 0, True)
            gate_up(0, 0, 1, True)
            gate_up(0, 1, 0)
            lora_t_down(0, 0, first=True)
            gate_up(0, 1, 1)
            with pe.Fori(1, FT // 2) as i:
                for u in range(2):
                    gate_up(i, u, 0)
                    lora_t_down(i + u - 1, 1 - u)
                    gate_up(i, u, 1)
            gate_up(FT // 2, 0, 0)
            lora_t_down(FT // 2 - 1, 1)
            gate_up(FT // 2, 0, 1)

            def down_base(m, h, cols=slice(0, HALF)):
                bank = down_bank(m, h, cols)
                if m < 2:
                    pe.wait_ge(silu_done, HSTEPS - 1 + m)
                    pe.wait_ge(act_lo_done, HSTEPS - 1 + m)
                else:
                    pe.wait_ge(y_done, NH * (m - 2) + h + 1)
                pe.wait_ge(wd_lo_done, m + 1)
                for f in range(FT):
                    rows = F_LAST if f == FT - 1 else P
                    if m == 0 and f == FT - 1:
                        pe.wait_ge(act_lo_done, HSTEPS - 1 + h)
                    at = slice(f * TOKENS + h * HALF + cols.start, f * TOKENS + h * HALF + cols.stop)
                    three_passes(ps[:, bank, cols], wd_hi[m % 2][0:rows, f, :], wd_lo[m % 2][0:rows, f, :],
                                 act_hi[0:rows, at], act_lo[0:rows, at], start=(f == 0))

            def down_lora(m, h, gls=range(GH)):
                bank = down_bank(m, h, slice(gls[0] * GT, HALF))
                pe.wait_ge(td_lo_done, NH)
                pe.wait_ge(bd_lo_done, 1)
                for gl in gls:
                    g = h * GH + gl
                    b = (slice(None), g, slice(m * P, (m + 1) * P))
                    last = three_passes(ps[:, bank, gl * GT:(gl + 1) * GT], bd_hi[b], bd_lo[b],
                                        td_hi[:, group_tokens(g)], td_lo[:, group_tokens(g)],
                                        stop=(gl == gls[-1]))
                last.then_inc(down_done, 1)

            down_base(0, 0)
            lora_t_down(FT // 2, 0, last_tile=True)
            down_base(0, 1)
            for h in range(NH):
                down_lora(0, h)
            for m in range(1, KT):
                for h in range(NH):
                    if (m, h) == (KT - 1, NH - 1):
                        for gl in range(GH):
                            down_base(m, h, LAST_COLS[gl])
                            down_lora(m, h, [gl])
                    else:
                        down_base(m, h)
                        down_lora(m, h)


def kernel(**inputs):
    import numpy as np
    import concourse.bacc as bacc
    from concourse.bass_utils import run_bass_kernel_spmd

    a = {k: np.asarray(v) for k, v in inputs.items()}
    c = np.ascontiguousarray

    def f_tiles(w):
        order = np.concatenate([np.arange((FT - 1) * P, F), np.arange(F - P, F - F_LAST)])
        return np.stack([w[..., f * P:(f + 1) * P] for f in range(FT - 1)] + [w[..., order]], axis=-2)

    xT = c(a["x"].reshape(NH, HALF, KT, P).transpose(0, 2, 3, 1))
    w0T = c(a["L0_cond_W"].T.reshape(KT, P, D))
    ar = np.concatenate([a["L0_cond_A"].reshape(ER0, D), a["L0_cond_Wr"]], axis=0)
    ar0T = c(ar.T.reshape(KT, P, HC).transpose(1, 0, 2))
    b0T = c(a["L0_cond_B"].transpose(0, 2, 1).reshape(ER0, D))

    consts = np.zeros((P, C_END), np.float32)
    block = np.arange(P)[:, None] // R1 == np.arange(GT)[None, :] // BATCH_TOKENS
    consts[:, C_MASK:C_MASK + GT] = np.where(block, 0.5, 0.0)
    consts[:, C_ID:C_ID + P] = np.eye(P)
    consts[:, C_IOTA:C_IOTA + E0] = np.arange(E0)
    consts[:, C_FTOFF:C_FTOFF + FT * NG] = np.repeat(np.arange(FT) * E1 * R1, NG)
    consts[:, C_ROFF] = np.arange(P) % R1

    lang = np.repeat(a["itok_B_0_7"], BATCH_TOKENS).reshape(NH * TT, P).T
    expert = np.repeat(a["itok_B_2_6"], R1).reshape(NG, P).T
    batches = np.broadcast_to(a["itok_B_2_6"], (P, NH * HB))
    ids = c(np.concatenate([lang, expert, batches], axis=1))

    gu = np.stack([f_tiles(a["L1_cond_W_gate"].T), f_tiles(a["L1_cond_W_up"].T)])
    wgu = c(gu.reshape(2, KT, P, FT, P).transpose(3, 2, 0, 1, 4).reshape(FT, P, 2 * KT * P))
    ga = np.stack([a["L1_cond_A_gate"][0], a["L1_cond_A_up"][0]])
    a_experts = c(ga.reshape(2, E1, R1, KT, P).transpose(1, 4, 3, 0, 2).reshape(E1, P, AW))
    parts = [f_tiles(a[n][0].transpose(0, 2, 1).reshape(E1 * R1, F)) for n in ("L1_cond_B_gate", "L1_cond_B_up")]
    ft_rows = c(np.stack(parts, axis=2).transpose(1, 0, 2, 3).reshape(FT * E1 * R1, GW))
    ad = f_tiles(a["L1_cond_A_down"][0]).transpose(0, 3, 2, 1).reshape(E1, P, FT * R1)
    ad_experts = np.split(ad, [AD_CHUNKS[0] * R1], axis=2)
    wd = c(f_tiles(a["L1_cond_W_down"]).reshape(KT, P, FT, P).transpose(0, 3, 2, 1).reshape(KT, P, FT * P))
    bd_rows = c(a["L1_cond_B_down"][0].transpose(0, 2, 1).reshape(E1 * R1, D))

    arrays = {"in_xT": xT, "in_w0T": w0T, "in_ar0T": ar0T, "in_b0T": b0T, "in_consts": consts, "in_ids": ids,
              "in_wgu": wgu, "in_a_experts": a_experts, "in_ft_rows": ft_rows,
              "in_ad_experts0": c(ad_experts[0]), "in_ad_experts1": c(ad_experts[1]),
              "in_wd": wd, "in_bd_rows": bd_rows}
    nc = bacc.Bacc("TRN2", target_bir_lowering=False, num_devices=1)
    aps = [nc.dram_tensor(n, v.shape, mybir.dt.from_np(v.dtype), kind="ExternalInput").ap()
           for n, v in arrays.items()]
    out = nc.dram_tensor("out_yT", (KT, NH, P, HALF), F32, kind="ExternalOutput").ap()
    mlp_with_loras(nc, *aps, out)
    r = run_bass_kernel_spmd(nc, [arrays], core_ids=[0])
    y = r.results[0]["out_yT"]
    return c(y.transpose(1, 3, 0, 2)).reshape(a["x"].shape)
```
